# Optimizing a Trainium2 kernel written in Bass

```python
import numpy as np
import jax
import jax.numpy as jnp

def _softmax(x, axis=-1):
    return jax.nn.softmax(x, axis=axis)

def _gelu(x):
    return jax.nn.gelu(x, approximate=True)

def _silu(x):
    return jax.nn.silu(x)

def _sigmoid(x):
    return jax.nn.sigmoid(x)

def _layernorm(x, axis=-1, eps=1e-05):
    m = jnp.mean(x, axis=axis, keepdims=True)
    v = jnp.var(x, axis=axis, keepdims=True)
    return (x - m) / jnp.sqrt(v + eps)

def _scatter_add(tgt, idx, src, axis=0):
    return tgt.at[idx].add(src)

def _segment_sum(src, seg, n):
    return jax.ops.segment_sum(src, seg, n)
kernel_name = 'mk_dlrm_tower_d1_rec_r8_75e179'

def setup_inputs(seed: int=0):
    np.random.seed(seed)
    _w = jnp.asarray

    def _rec_inputs():
        import jax
        import jax.numpy as jnp
        _tk = jax.random.key(seed)
        dense_ctx = jax.random.normal(jax.random.fold_in(_tk, 190), (2048, 16), jnp.float32)
        ids = jnp.stack([jax.random.randint(jax.random.fold_in(_tk, 200 + f), (2048,), 0, v, jnp.int32) for f, v in enumerate([12500, 125000, 1000, 1000, 1250, 1250, 125000, 1250, 1250, 1250, 1250, 12500, 1000, 1250, 125000, 1250, 1250, 1000, 1250, 1000, 12500, 12500, 125000, 12500, 1000, 1250, 1250, 125000, 125000, 12500, 125000, 1250, 1000, 1000, 1000, 1000, 1000, 1000, 1000, 1000])], axis=1)
        tbl_0 = 0.05 * jax.random.normal(jax.random.fold_in(_tk, 500 + 0), (12500, 32), jnp.float32)
        tbl_1 = 0.05 * jax.random.normal(jax.random.fold_in(_tk, 500 + 1), (125000, 32), jnp.float32)
        tbl_2 = 0.05 * jax.random.normal(jax.random.fold_in(_tk, 500 + 2), (1000, 32), jnp.float32)
        tbl_3 = 0.05 * jax.random.normal(jax.random.fold_in(_tk, 500 + 3), (1000, 32), jnp.float32)
        tbl_4 = 0.05 * jax.random.normal(jax.random.fold_in(_tk, 500 + 4), (1250, 32), jnp.float32)
        tbl_5 = 0.05 * jax.random.normal(jax.random.fold_in(_tk, 500 + 5), (1250, 32), jnp.float32)
        tbl_6 = 0.05 * jax.random.normal(jax.random.fold_in(_tk, 500 + 6), (125000, 32), jnp.float32)
        tbl_7 = 0.05 * jax.random.normal(jax.random.fold_in(_tk, 500 + 7), (1250, 32), jnp.float32)
        tbl_8 = 0.05 * jax.random.normal(jax.random.fold_in(_tk, 500 + 8), (1250, 32), jnp.float32)
        tbl_9 = 0.05 * jax.random.normal(jax.random.fold_in(_tk, 500 + 9), (1250, 32), jnp.float32)
        tbl_10 = 0.05 * jax.random.normal(jax.random.fold_in(_tk, 500 + 10), (1250, 32), jnp.float32)
        tbl_11 = 0.05 * jax.random.normal(jax.random.fold_in(_tk, 500 + 11), (12500, 32), jnp.float32)
        tbl_12 = 0.05 * jax.random.normal(jax.random.fold_in(_tk, 500 + 12), (1000, 32), jnp.float32)
        tbl_13 = 0.05 * jax.random.normal(jax.random.fold_in(_tk, 500 + 13), (1250, 32), jnp.float32)
        tbl_14 = 0.05 * jax.random.normal(jax.random.fold_in(_tk, 500 + 14), (125000, 32), jnp.float32)
        tbl_15 = 0.05 * jax.random.normal(jax.random.fold_in(_tk, 500 + 15), (1250, 32), jnp.float32)
        tbl_16 = 0.05 * jax.random.normal(jax.random.fold_in(_tk, 500 + 16), (1250, 32), jnp.float32)
        tbl_17 = 0.05 * jax.random.normal(jax.random.fold_in(_tk, 500 + 17), (1000, 32), jnp.float32)
        tbl_18 = 0.05 * jax.random.normal(jax.random.fold_in(_tk, 500 + 18), (1250, 32), jnp.float32)
        tbl_19 = 0.05 * jax.random.normal(jax.random.fold_in(_tk, 500 + 19), (1000, 32), jnp.float32)
        tbl_20 = 0.05 * jax.random.normal(jax.random.fold_in(_tk, 500 + 20), (12500, 32), jnp.float32)
        tbl_21 = 0.05 * jax.random.normal(jax.random.fold_in(_tk, 500 + 21), (12500, 32), jnp.float32)
        tbl_22 = 0.05 * jax.random.normal(jax.random.fold_in(_tk, 500 + 22), (125000, 32), jnp.float32)
        tbl_23 = 0.05 * jax.random.normal(jax.random.fold_in(_tk, 500 + 23), (12500, 32), jnp.float32)
        tbl_24 = 0.05 * jax.random.normal(jax.random.fold_in(_tk, 500 + 24), (1000, 32), jnp.float32)
        tbl_25 = 0.05 * jax.random.normal(jax.random.fold_in(_tk, 500 + 25), (1250, 32), jnp.float32)
        tbl_26 = 0.05 * jax.random.normal(jax.random.fold_in(_tk, 500 + 26), (1250, 32), jnp.float32)
        tbl_27 = 0.05 * jax.random.normal(jax.random.fold_in(_tk, 500 + 27), (125000, 32), jnp.float32)
        tbl_28 = 0.05 * jax.random.normal(jax.random.fold_in(_tk, 500 + 28), (125000, 32), jnp.float32)
        tbl_29 = 0.05 * jax.random.normal(jax.random.fold_in(_tk, 500 + 29), (12500, 32), jnp.float32)
        tbl_30 = 0.05 * jax.random.normal(jax.random.fold_in(_tk, 500 + 30), (125000, 32), jnp.float32)
        tbl_31 = 0.05 * jax.random.normal(jax.random.fold_in(_tk, 500 + 31), (1250, 32), jnp.float32)
        tbl_32 = 0.05 * jax.random.normal(jax.random.fold_in(_tk, 500 + 32), (1000, 32), jnp.float32)
        tbl_33 = 0.05 * jax.random.normal(jax.random.fold_in(_tk, 500 + 33), (1000, 32), jnp.float32)
        tbl_34 = 0.05 * jax.random.normal(jax.random.fold_in(_tk, 500 + 34), (1000, 32), jnp.float32)
        tbl_35 = 0.05 * jax.random.normal(jax.random.fold_in(_tk, 500 + 35), (1000, 32), jnp.float32)
        tbl_36 = 0.05 * jax.random.normal(jax.random.fold_in(_tk, 500 + 36), (1000, 32), jnp.float32)
        tbl_37 = 0.05 * jax.random.normal(jax.random.fold_in(_tk, 500 + 37), (1000, 32), jnp.float32)
        tbl_38 = 0.05 * jax.random.normal(jax.random.fold_in(_tk, 500 + 38), (1000, 32), jnp.float32)
        tbl_39 = 0.05 * jax.random.normal(jax.random.fold_in(_tk, 500 + 39), (1000, 32), jnp.float32)
        _rk = jax.random.fold_in(_tk, 7)
        W_top1 = 0.176777 * jax.random.normal(jax.random.fold_in(_tk, 801), (32, 512), jnp.float32)
        W_top2 = 0.0441942 * jax.random.normal(jax.random.fold_in(_tk, 802), (512, 256), jnp.float32)
        W_top3 = 0.0625 * jax.random.normal(jax.random.fold_in(_tk, 803), (256, 1), jnp.float32)
        b_top1 = jnp.zeros((512,), jnp.float32)
        b_top2 = jnp.zeros((256,), jnp.float32)
        return (dense_ctx, ids, tbl_0, tbl_1, tbl_2, tbl_3, tbl_4, tbl_5, tbl_6, tbl_7, tbl_8, tbl_9, tbl_10, tbl_11, tbl_12, tbl_13, tbl_14, tbl_15, tbl_16, tbl_17, tbl_18, tbl_19, tbl_20, tbl_21, tbl_22, tbl_23, tbl_24, tbl_25, tbl_26, tbl_27, tbl_28, tbl_29, tbl_30, tbl_31, tbl_32, tbl_33, tbl_34, tbl_35, tbl_36, tbl_37, tbl_38, tbl_39, W_top1, b_top1, W_top2, b_top2, W_top3)
    dense_ctx, ids, tbl_0, tbl_1, tbl_2, tbl_3, tbl_4, tbl_5, tbl_6, tbl_7, tbl_8, tbl_9, tbl_10, tbl_11, tbl_12, tbl_13, tbl_14, tbl_15, tbl_16, tbl_17, tbl_18, tbl_19, tbl_20, tbl_21, tbl_22, tbl_23, tbl_24, tbl_25, tbl_26, tbl_27, tbl_28, tbl_29, tbl_30, tbl_31, tbl_32, tbl_33, tbl_34, tbl_35, tbl_36, tbl_37, tbl_38, tbl_39, W_top1, b_top1, W_top2, b_top2, W_top3 = _rec_inputs()

    def _L0_rec_setup():
        import jax, jax.numpy as jnp
        import numpy as np
        import itertools
        LN_EPS = 0.001

        def _pair_indices(field_num):
            pairs = np.array(list(itertools.combinations(range(field_num), 2)), dtype=np.int32)
            return (pairs[:, 0], pairs[:, 1])
        key = jax.random.key(seed)
        ks = jax.random.split(key, 3)
        B, F, E, P, D = (256, 40, 32, 780, 16)
        x = jax.random.normal(ks[0], (B, F, E), dtype=jnp.float32)
        W = jax.random.normal(ks[1], (P, E, E), dtype=jnp.float32) * (2.0 / (E + E)) ** 0.5
        dense_w = jax.random.normal(ks[2], (P, D), dtype=jnp.float32) * (2.0 / (P + D)) ** 0.5
        dense_b = jnp.zeros((D,), dtype=jnp.float32)
        gamma = jnp.ones((D,), dtype=jnp.float32)
        beta = jnp.zeros((D,), dtype=jnp.float32)
        return {'x': x, 'W': W, 'dense_w': dense_w, 'dense_b': dense_b, 'gamma': gamma, 'beta': beta}
    _L0_rec_all = _L0_rec_setup()
    _L0_rec_in = {k: v for k, v in _L0_rec_all.items() if k in ('W', 'dense_w', 'dense_b', 'gamma', 'beta')}
    del _L0_rec_all
    return {'dense_ctx': dense_ctx, 'ids': ids, 'tbl_0': tbl_0, 'tbl_1': tbl_1, 'tbl_2': tbl_2, 'tbl_3': tbl_3, 'tbl_4': tbl_4, 'tbl_5': tbl_5, 'tbl_6': tbl_6, 'tbl_7': tbl_7, 'tbl_8': tbl_8, 'tbl_9': tbl_9, 'tbl_10': tbl_10, 'tbl_11': tbl_11, 'tbl_12': tbl_12, 'tbl_13': tbl_13, 'tbl_14': tbl_14, 'tbl_15': tbl_15, 'tbl_16': tbl_16, 'tbl_17': tbl_17, 'tbl_18': tbl_18, 'tbl_19': tbl_19, 'tbl_20': tbl_20, 'tbl_21': tbl_21, 'tbl_22': tbl_22, 'tbl_23': tbl_23, 'tbl_24': tbl_24, 'tbl_25': tbl_25, 'tbl_26': tbl_26, 'tbl_27': tbl_27, 'tbl_28': tbl_28, 'tbl_29': tbl_29, 'tbl_30': tbl_30, 'tbl_31': tbl_31, 'tbl_32': tbl_32, 'tbl_33': tbl_33, 'tbl_34': tbl_34, 'tbl_35': tbl_35, 'tbl_36': tbl_36, 'tbl_37': tbl_37, 'tbl_38': tbl_38, 'tbl_39': tbl_39, 'W_top1': W_top1, 'b_top1': b_top1, 'W_top2': W_top2, 'b_top2': b_top2, 'W_top3': W_top3, 'L0_rec_W': _L0_rec_in['W'], 'L0_rec_dense_w': _L0_rec_in['dense_w'], 'L0_rec_dense_b': _L0_rec_in['dense_b'], 'L0_rec_gamma': _L0_rec_in['gamma'], 'L0_rec_beta': _L0_rec_in['beta']}

def reference(dense_ctx, ids, tbl_0, tbl_1, tbl_2, tbl_3, tbl_4, tbl_5, tbl_6, tbl_7, tbl_8, tbl_9, tbl_10, tbl_11, tbl_12, tbl_13, tbl_14, tbl_15, tbl_16, tbl_17, tbl_18, tbl_19, tbl_20, tbl_21, tbl_22, tbl_23, tbl_24, tbl_25, tbl_26, tbl_27, tbl_28, tbl_29, tbl_30, tbl_31, tbl_32, tbl_33, tbl_34, tbl_35, tbl_36, tbl_37, tbl_38, tbl_39, W_top1, b_top1, W_top2, b_top2, W_top3, L0_rec_W, L0_rec_dense_w, L0_rec_dense_b, L0_rec_gamma, L0_rec_beta):
    import jax
    import jax.numpy as jnp

    def _L0_rec_ref(x, W, dense_w, dense_b, gamma, beta):
        import jax, jax.numpy as jnp
        import numpy as np
        import itertools
        LN_EPS = 0.001

        def _pair_indices(field_num):
            pairs = np.array(list(itertools.combinations(range(field_num), 2)), dtype=np.int32)
            return (pairs[:, 0], pairs[:, 1])
        F = x.shape[1]
        idx_i, idx_j = _pair_indices(F)
        xi = x[:, idx_i, :]
        xj = x[:, idx_j, :]
        t = jnp.einsum('bpe,pef->bpf', xi, W)
        p = jnp.einsum('bpf,bpf->bp', t, xj)
        h = p @ dense_w + dense_b
        mu = jnp.mean(h, axis=-1, keepdims=True)
        var = jnp.mean(jnp.square(h - mu), axis=-1, keepdims=True)
        out = (h - mu) * jax.lax.rsqrt(var + LN_EPS) * gamma + beta
        return out
    e = jnp.stack([tbl_0[ids[:, 0]], tbl_1[ids[:, 1]], tbl_2[ids[:, 2]], tbl_3[ids[:, 3]], tbl_4[ids[:, 4]], tbl_5[ids[:, 5]], tbl_6[ids[:, 6]], tbl_7[ids[:, 7]], tbl_8[ids[:, 8]], tbl_9[ids[:, 9]], tbl_10[ids[:, 10]], tbl_11[ids[:, 11]], tbl_12[ids[:, 12]], tbl_13[ids[:, 13]], tbl_14[ids[:, 14]], tbl_15[ids[:, 15]], tbl_16[ids[:, 16]], tbl_17[ids[:, 17]], tbl_18[ids[:, 18]], tbl_19[ids[:, 19]], tbl_20[ids[:, 20]], tbl_21[ids[:, 21]], tbl_22[ids[:, 22]], tbl_23[ids[:, 23]], tbl_24[ids[:, 24]], tbl_25[ids[:, 25]], tbl_26[ids[:, 26]], tbl_27[ids[:, 27]], tbl_28[ids[:, 28]], tbl_29[ids[:, 29]], tbl_30[ids[:, 30]], tbl_31[ids[:, 31]], tbl_32[ids[:, 32]], tbl_33[ids[:, 33]], tbl_34[ids[:, 34]], tbl_35[ids[:, 35]], tbl_36[ids[:, 36]], tbl_37[ids[:, 37]], tbl_38[ids[:, 38]], tbl_39[ids[:, 39]]], axis=1)
    z = _L0_rec_ref(e, L0_rec_W, L0_rec_dense_w, L0_rec_dense_b, L0_rec_gamma, L0_rec_beta)
    z = z.reshape(z.shape[0], -1)
    h = jnp.concatenate([z, dense_ctx], axis=1)
    h = jnp.maximum(h @ W_top1 + b_top1, 0.0)
    h = jnp.maximum(h @ W_top2 + b_top2, 0.0)
    y = h @ W_top3
    return y

_drawn_inputs = setup_inputs


def setup_inputs(seed=0):
    import zlib

    import numpy as np

    out = dict(_drawn_inputs(seed))
    spreads = {'b_top1': (0.0, 0.1),
     'b_top2': (0.0, 0.1),
     'L0_rec_dense_b': (0.0, 0.1),
     'L0_rec_gamma': (1.0, 0.2),
     'L0_rec_beta': (0.0, 0.1)}
    factors = {}
    for name, (base, spread) in spreads.items():
        noise = np.random.default_rng([zlib.crc32(name.encode()), seed]).standard_normal(out[name].shape)
        drawn = base * np.exp(spread * noise) if base else spread * noise
        out[name] = jnp.asarray(drawn.astype(out[name].dtype))
    for name, factor in factors.items():
        out[name] = (out[name] * factor).astype(out[name].dtype)
    return out
```

```python
import concourse.bass as bass
import concourse.mybir as mybir
from concourse.alu_op_type import AluOpType as ALU
from contextlib import ExitStack

F32 = mybir.dt.float32
F32R = mybir.dt.float32r
I32 = mybir.dt.int32
ACT = mybir.ActivationFunctionType
AX = mybir.AxisListType

FIELDS, EMB, DENSE, BATCH = 40, 32, 16, 2048
LN_EPS = 1e-3
SLOTS = 4
GROUPS = FIELDS // SLOTS
CB = 256
BT = CB // 128
CHUNKS = BATCH // CB
GATHERS = SLOTS * BT
HID1, HID2 = 512, 256
M1, M2 = HID1 // 128, HID2 // 128
TILE = SLOTS * EMB
DIAG_B = 9 * EMB
STAGE = 1600


def position_order():
    return list(range(FIELDS))


def batches_of_chunk():
    out = []
    for step in range(GROUPS):
        q = GROUPS - 1 - step
        if step % 2:
            out.append(("diag", q, q, step))
        out += [("full", q, k, step) for k in range(q + 1, GROUPS)]
    return out


BATCHES = batches_of_chunk()
NB = len(BATCHES)
W_WIDTH = {"full": SLOTS * TILE, "diag": 2 * (TILE + DIAG_B)}
W_START = [sum(W_WIDTH[b[0]] for b in BATCHES[:n]) for n in range(NB + 1)]
W_COLS = W_START[-1]
PIECES = W_COLS // STAGE
assert PIECES * STAGE == W_COLS and NB == 50
DIAG_WINDOW = {1: 0, 2: 2, 3: 5}
DIAG_SOURCE = {1: 3, 2: 1, 3: 2}


def first_batch(step):
    return min([n for n, b in enumerate(BATCHES) if b[3] == step], default=None)


def last_batch(step):
    if step % 2 == 0:
        return first_batch(step + 1)
    return max(n for n, b in enumerate(BATCHES) if b[3] == step)


U_RING = 3


def u_previous(b):
    slot = b % U_RING
    n = b - 1
    while (n % NB) % U_RING != slot:
        n -= 1
    return b - n


def places():
    prep, tp = {}, {}
    for step in range(2, GROUPS + 2):
        own = [n for n, b in enumerate(BATCHES) if b[3] == min(step - 1, GROUPS - 1)]
        a = own[0] + len(own) // 2 - 1
        if step == GROUPS:
            a = own[0] + 1
        if step == GROUPS + 1:
            a = own[-1] - 3
        prep.setdefault(a, []).append(step)
        tp.setdefault(own[-1] if step == GROUPS + 1 else min(a + 2, own[-1]), []).append(step)
    return prep, tp


PREP_AT, TP_AT = places()
HSUM_AT = 1
MLP_STEPS = 2 + M1 + M2 + 1
MLP_AT = {3: 0, 18: 1, **{20 + 2 * m: 2 + m for m in range(M1 + M2 + 1)}}
LN_OPS = 10
ROOT_OP = 5
LN_AT = {5 + n + (2 if n > ROOT_OP else 0): n for n in range(LN_OPS)}
ROOT_AT = 5 + ROOT_OP + 1
assert max(MLP_AT) < NB - 2


def tower(nc, ids, dense_ctx, tables, w_pairs, dense_w, dense_b, gamma, beta, eye, group_sum,
          w1, b1, w2, b2, w3, out):
    order = position_order()
    ctx = ExitStack()
    with ctx:
        def sb(name, shape, dt=F32):
            return ctx.enter_context(nc.sbuf_tensor(name, shape, dt))

        def sem(name):
            return ctx.enter_context(nc.semaphore(name))

        w_stack = sb("w_stack", [128, W_COLS], F32R)
        w_stage = sb("w_stage", [128, 2, STAGE])
        dw = sb("dw", [128, NB * SLOTS, DENSE])
        index = sb("index", [128, GROUPS * GATHERS], I32)
        x_rows = sb("x_rows", [128, GROUPS, BT, TILE])
        x_halves = sb("x_halves", [128, 2, BT * SLOTS, 2, 2, EMB])
        x_stack = sb("x_stack", [128, 2, SLOTS, CB], F32R)
        x_cols = sb("x_cols", [128, 2 * GROUPS, CB])
        u = sb("u", [128, U_RING, SLOTS, CB])
        ident = sb("ident", [128, 128])
        gsum = sb("gsum", [128, DENSE])
        ones = sb("ones", [1, 128])
        db_row = sb("db_row", [1, DENSE])
        gamma_b = sb("gamma_b", [128, DENSE])
        beta_b = sb("beta_b", [128, DENSE])
        w1_sb = sb("w1_sb", [2 * DENSE, HID1])
        w2_sb = sb("w2_sb", [128, M1, HID2])
        w3_sb = sb("w3_sb", [128, M2])
        b1_sb = sb("b1_sb", [128, M1])
        b2_sb = sb("b2_sb", [128, M2])
        h_sums = sb("h_sums", [128, CB])
        ln_sum = sb("ln_sum", [128, BT])
        ln_mean = sb("ln_mean", [128, BT])
        ln_cent = sb("ln_cent", [128, BT, DENSE])
        ln_sq = sb("ln_sq", [128, BT, DENSE])
        ln_var = sb("ln_var", [128, BT])
        ln_ve = sb("ln_ve", [128, BT])
        ln_root = sb("ln_root", [128, BT])
        ln_rstd = sb("ln_rstd", [128, BT])
        ln_z = sb("ln_z", [128, BT, DENSE])
        ln_g = sb("ln_g", [128, BT, DENSE])
        z_rows = sb("z_rows", [128, BT, 2 * DENSE])
        z_cols = sb("z_cols", [2 * DENSE, CB])
        hid1 = sb("hid1", [128, M1, CB])
        hid2 = sb("hid2", [128, M2, CB])
        y_row = sb("y_row", [1, CB])

        t_ps = ctx.enter_context(nc.psum_tensor("t_ps", [128, 2, SLOTS, CB], F32))
        stack_ps = ctx.enter_context(nc.psum_tensor("stack_ps", [128, SLOTS, CB], F32))
        mlp_bank = ctx.enter_context(nc.psum_tensor("mlp_bank", [128, 512], F32))
        h_ps = ctx.enter_context(nc.psum_tensor("h_ps", [128, 512], F32))
        cols_ps = stack_ps[:, 0, :]
        mlp_ps = mlp_bank[:, 0:CB]

        index_hi, index_lo = sem("index_hi"), sem("index_lo")
        gathered = [sem(f"gathered{s}") for s in range(GROUPS)]
        staged = [sem(f"staged{i}") for i in range(2)]
        dw_in, ident_in, mlp_in = sem("dw_in"), sem("ident_in"), sem("mlp_in")
        gather_turn = sem("gather_turn")
        dense_in, y_out = sem("dense_in"), sem("y_out")
        w_hi, w_lo = sem("w_hi"), sem("w_lo")
        x_hi, x_lo, x_dup = sem("x_hi"), sem("x_lo"), sem("x_dup")
        cols_tp, stack_tp = sem("cols_tp"), sem("stack_tp")
        cols_ok, stack_ok = sem("cols_ok"), sem("stack_ok")
        t_ok, u_ok, summed = sem("t_ok"), sem("u_ok"), sem("summed")
        h_out = sem("h_out")
        memset_ok = sem("memset_ok")
        mlp_mm, mlp_act, ln_op, root = sem("mlp_mm"), sem("mlp_act"), sem("ln_op"), sem("root")

        block = ctx.enter_context(nc.Block())

        def batch_no(c, b):
            return c * NB + b + 1

        def group_no(c, step):
            return c * GROUPS + step + 1

        def mlp_no(c, n):
            return c * MLP_STEPS + n + 1

        def pieces_before(b):
            return min(PIECES, -(-W_START[b + 1] // STAGE) + 2)

        @block.gpsimd
        def _(pool):
            def gather(c, step):
                if step == 0:
                    pool.wait_ge(index_hi, 16 * (c + 1))
                if step == GROUPS // 2:
                    pool.wait_ge(index_lo, 16 * (c + 1))
                if not isinstance(c, int):
                    pool.wait_ge(stack_tp, group_no(c - 1, step))
                    pool.sem_inc(gather_turn, 1)
                for r in range(SLOTS):
                    table = tables[order[SLOTS * (GROUPS - 1 - step) + r]]
                    for bt in range(BT):
                        n = step * GATHERS + r * BT + bt
                        pool.indirect_dma_start(
                            x_rows[:, step, bt, r * EMB:(r + 1) * EMB], None, table,
                            bass.IndirectOffsetOnAxis(ap=index[:, n:n + 1], axis=0),
                        ).then_inc(gathered[step], 16)

            for step in range(GROUPS):
                gather(0, step)
            with pool.Fori(1, CHUNKS) as c:
                for step in range(GROUPS):
                    gather(c, step)

        @block.sync
        def _(sp):
            half = GROUPS // 2 * GATHERS

            def load_indices(c, lo):
                if not isinstance(c, int) or c > 0:
                    for step in range(lo * GROUPS // 2, (lo + 1) * GROUPS // 2):
                        sp.wait_ge(gathered[step], 16 * GATHERS * c)
                src = ids[bass.ds(c, 1)].rearrange("a p n -> p (a n)")
                sp.dma_start(index[:, lo * half:(lo + 1) * half],
                             src[:, lo * half:(lo + 1) * half]).then_inc(index_lo if lo else index_hi, 16)

            def load_piece(n):
                if n >= 2:
                    sp.wait_ge(w_lo, n - 1)
                for part in range(4):
                    sp.dma_start(w_stage[part * EMB:(part + 1) * EMB, n % 2, :],
                                 w_pairs[:, n * STAGE:(n + 1) * STAGE]).then_inc(staged[n % 2], 16)

            load_indices(0, 0)
            load_indices(0, 1)
            sp.dma_start(ident[:, :], eye).then_inc(ident_in, 16)
            for n in range(PIECES):
                load_piece(n)
                if n == PIECES * 2 // 3:
                    load_indices(1, 0)
            load_indices(1, 1)
            with sp.Fori(2, CHUNKS) as c:
                load_indices(c, 0)
                load_indices(c, 1)

        @block.scalar
        def _(act):
            def split_piece(n):
                act.wait_ge(staged[n % 2], 64 * (n // 2 + 1))
                nc.scalar.activation(w_stack[:, n * STAGE:(n + 1) * STAGE], w_stage[:, n % 2, :],
                                     ACT.Copy).then_inc(w_hi, 1)

            def halves(c, step, parity):
                own = x_halves[:, step % 2]
                q_rows = x_rows[:, step, :, :].rearrange("p b (s e) -> p (b s) e", e=EMB)
                act.wait_ge(gathered[step], 16 * GATHERS * (c + 1))
                if not isinstance(c, int) or c * GROUPS + step >= 2:
                    act.wait_ge(stack_tp, group_no(c, step) - 2)
                nc.scalar.activation(own[:, :, :, 0, :].bitcast(F32R),
                                     q_rows.unsqueeze(2).to_broadcast([128, BT * SLOTS, 2, EMB]),
                                     ACT.Copy).then_inc(x_hi, 1)
                act.wait_ge(cols_tp, group_no(c, step))
                nc.scalar.activation(
                    x_cols[:, bass.ds(parity * GROUPS + GROUPS - 1 - step, 1), :].rearrange("p a n -> p (a n)"),
                    cols_ps, ACT.Copy).then_inc(cols_ok, 1)
                act.wait_ge(x_lo, group_no(c, step))
                nc.scalar.activation(own[:, :, 1, 1, :].bitcast(F32R), own[:, :, 0, 1, :].bitcast(F32R),
                                     ACT.Copy).then_inc(x_dup, 1)

            def stack(c, step):
                act.wait_ge(stack_tp, group_no(c, step))
                if step >= 2:
                    act.wait_ge(t_ok, batch_no(c, last_batch(step - 2)))
                elif not isinstance(c, int) or c > 0:
                    act.wait_ge(t_ok, batch_no(c - 1, last_batch(GROUPS - 2 + step)))
                nc.scalar.activation(x_stack[:, step % 2], stack_ps[:, :, :], ACT.Copy).then_inc(stack_ok, 1)

            def sums_out(c):
                act.wait_ge(summed, batch_no(c, NB - 1))
                for g in range(SLOTS):
                    last = nc.scalar.activation(h_sums[32 * g:32 * g + DENSE, :],
                                                h_ps[32 * g:32 * g + DENSE, 0:CB], ACT.Copy)
                    last.then_inc(h_out, 1)

            def load_dense(c):
                act.dma_start(z_rows[:, :, DENSE:2 * DENSE],
                              dense_ctx[bass.ds(c, 1)].rearrange("a (b p) n -> p (a b) n", p=128))\
                   .then_inc(dense_in, 16)

            def norm_root(c):
                act.wait_ge(ln_op, c * LN_OPS + ROOT_OP + 1)
                nc.scalar.activation(ln_root[:, :], ln_ve[:, :], ACT.Sqrt).then_inc(root, 1)

            def mlp_step(c, n):
                if n == 0:
                    return
                act.wait_ge(mlp_mm, mlp_no(c, n))
                if n == 1:
                    nc.scalar.activation(z_cols[:, :], mlp_ps[0:2 * DENSE, :], ACT.Copy).then_inc(mlp_act, 1)
                elif n < 2 + M1:
                    m = n - 2
                    nc.scalar.activation(hid1[:, m, :], mlp_ps, ACT.Relu, bias=b1_sb[:, m:m + 1])\
                      .then_inc(mlp_act, 1)
                elif n < 2 + M1 + M2:
                    m = n - 2 - M1
                    nc.scalar.activation(hid2[:, m, :], mlp_ps, ACT.Relu, bias=b2_sb[:, m:m + 1])\
                      .then_inc(mlp_act, 1)
                else:
                    nc.scalar.activation(y_row[:, :], mlp_ps[0:1, :], ACT.Copy).then_inc(mlp_act, 1)
                    act.wait_ge(mlp_act, (MLP_STEPS - 1) * (c + 1))
                    act.dma_start(out[bass.ds(c, 1), :], y_row[:, :]).then_inc(y_out, 16)

            def chunk(c, parity, before, after):
                pieces = 2
                for b in range(NB):
                    if before is None:
                        while pieces < pieces_before(b):
                            split_piece(pieces)
                            pieces += 1
                    elif b == HSUM_AT:
                        sums_out(before)
                        load_dense(before)
                    if before is not None and b == ROOT_AT:
                        norm_root(before)
                    if before is not None and b in MLP_AT:
                        mlp_step(before, MLP_AT[b])
                    for step in PREP_AT.get(b, []):
                        if step < GROUPS:
                            halves(c, step, parity)
                        elif after is not None:
                            halves(after, step - GROUPS, 1 - parity)
                    for step in TP_AT.get(b, []):
                        if step < GROUPS:
                            stack(c, step)
                        elif after is not None:
                            stack(after, step - GROUPS)
                if before is not None:
                    act.wait_ge(y_out, 16 * (before + 1))

            small = [(gsum[:, :], group_sum), (db_row[:, :], dense_b), (gamma_b[:, :], gamma.to_broadcast([128, DENSE])),
                     (beta_b[:, :], beta.to_broadcast([128, DENSE])), (w1_sb[:, :], w1),
                     (w2_sb[:, :, :], w2.rearrange("(k p) n -> p k n", p=128)),
                     (w3_sb[:, :], w3), (b1_sb[:, :], b1), (b2_sb[:, :], b2)]
            for s in range(SLOTS):
                act.dma_start(dw[s * EMB:(s + 1) * EMB, :, :],
                              dense_w[s:s + 1].to_broadcast([EMB, NB * SLOTS, DENSE])).then_inc(dw_in, 16)
            for dst, src in small:
                act.dma_start(dst, src).then_inc(mlp_in, 16)
            split_piece(0)
            split_piece(1)
            for step in range(2):
                halves(0, step, 0)
                stack(0, step)
            chunk(0, 0, None, 1)
            act.wait_ge(mlp_in, 16 * len(small))
            act.wait_ge(memset_ok, 2)
            with act.Fori(1, CHUNKS - 1) as c:
                chunk(c, c % 2, c - 1, c + 1)
            chunk(CHUNKS - 1, (CHUNKS - 1) % 2, CHUNKS - 2, None)
            sums_out(CHUNKS - 1)
            load_dense(CHUNKS - 1)
            norm_root(CHUNKS - 1)
            for n in range(MLP_STEPS):
                mlp_step(CHUNKS - 1, n)
            act.wait_ge(y_out, 16 * CHUNKS)

        @block.vector
        def _(dve):
            def split_piece(n):
                cols = w_stack[64:128, n * STAGE:(n + 1) * STAGE]
                dve.wait_ge(w_hi, n + 1)
                nc.vector.tensor_tensor(cols, w_stage[64:128, n % 2, :], cols, ALU.subtract).then_inc(w_lo, 1)

            def lo_half(c, step):
                own = x_halves[:, step % 2]
                rows = x_rows[:, step, :, :].rearrange("p b (s e) -> p (b s) e", e=EMB)
                dve.wait_ge(x_hi, group_no(c, step))
                nc.vector.tensor_tensor(own[:, :, 0, 1, :].bitcast(F32R), rows,
                                        own[:, :, 0, 0, :].bitcast(F32R), ALU.subtract).then_inc(x_lo, 1)

            def multiply(c, b, parity):
                kind, q, k, step = BATCHES[b]
                dve.wait_ge(t_ok, batch_no(c, b))
                if b == first_batch(step):
                    dve.wait_ge(cols_ok, group_no(c, step))
                if not isinstance(c, int) or c * NB + b >= U_RING:
                    dve.wait_ge(summed, batch_no(c, b) - u_previous(b))
                if kind == "full":
                    x = x_cols[:, bass.ds(parity * GROUPS + k, 1), :].to_broadcast([128, SLOTS, CB])
                    nc.vector.tensor_tensor(u[:, b % U_RING], t_ps[:, b % 2], x, ALU.mult).then_inc(u_ok, 1)
                else:
                    x = x_cols[:, bass.ds(parity * GROUPS + q, 2), :].unsqueeze(2).to_broadcast([128, 2, 2, CB])
                    nc.vector.tensor_tensor(u[:, b % U_RING].rearrange("p (g a) n -> p g a n", a=2),
                                            t_ps[:, b % 2].rearrange("p (g a) n -> p g a n", a=2),
                                            x, ALU.mult).then_inc(u_ok, 1)

            h_rows = mlp_ps[:, 0:BT * DENSE].rearrange("p (b d) -> p b d", d=DENSE)

            def over_rows(ap):
                return ap.unsqueeze(1).to_broadcast([128, BT, DENSE])

            def over_dense(ap):
                return ap.unsqueeze(2).to_broadcast([128, BT, DENSE])

            def norm_op(c, n):
                if n == 0:
                    dve.wait_ge(mlp_mm, mlp_no(c, 0))
                else:
                    dve.wait_ge(ln_op, c * LN_OPS + n)
                if n == 0:
                    op = nc.vector.tensor_reduce(ln_sum[:, :], h_rows, AX.X, ALU.add)
                elif n == 1:
                    op = nc.vector.tensor_scalar(ln_mean[:, :], ln_sum[:, :], 1.0 / DENSE, None, ALU.mult)
                elif n == 2:
                    op = nc.vector.tensor_tensor(ln_cent[:, :, :], h_rows, over_dense(ln_mean[:, :]), ALU.subtract)
                elif n == 3:
                    op = nc.vector.tensor_tensor(ln_sq[:, :, :], ln_cent[:, :, :], ln_cent[:, :, :], ALU.mult)
                elif n == 4:
                    op = nc.vector.tensor_reduce(ln_var[:, :], ln_sq[:, :, :], AX.X, ALU.add)
                elif n == 5:
                    op = nc.vector.tensor_scalar(ln_ve[:, :], ln_var[:, :], 1.0 / DENSE, LN_EPS, ALU.mult, ALU.add)
                elif n == 6:
                    dve.wait_ge(root, c + 1)
                    op = nc.vector.reciprocal(ln_rstd[:, :], ln_root[:, :])
                elif n == 7:
                    op = nc.vector.tensor_tensor(ln_z[:, :, :], ln_cent[:, :, :], over_dense(ln_rstd[:, :]), ALU.mult)
                elif n == 8:
                    op = nc.vector.tensor_tensor(ln_g[:, :, :], ln_z[:, :, :], over_rows(gamma_b[:, :]), ALU.mult)
                else:
                    op = nc.vector.tensor_tensor(z_rows[:, :, 0:DENSE], ln_g[:, :, :], over_rows(beta_b[:, :]), ALU.add)
                op.then_inc(ln_op, 1)

            def chunk(c, parity, before, after):
                pieces = 2
                for b in range(NB):
                    if before is None:
                        while pieces < pieces_before(b):
                            split_piece(pieces)
                            pieces += 1
                    multiply(c, b, parity)
                    if before is not None and b in LN_AT:
                        norm_op(before, LN_AT[b])
                    for step in PREP_AT.get(b, []):
                        if step < GROUPS:
                            lo_half(c, step)
                        elif after is not None:
                            lo_half(after, step - GROUPS)

            nc.vector.memset(h_sums[:, :], 0.0).then_inc(memset_ok, 1)
            nc.vector.memset(ones[:, :], 1.0).then_inc(memset_ok, 1)
            split_piece(0)
            split_piece(1)
            for step in range(2):
                lo_half(0, step)
            chunk(0, 0, None, 1)
            dve.wait_ge(mlp_in, 16 * 9)
            with dve.Fori(1, CHUNKS - 1) as c:
                chunk(c, c % 2, c - 1, c + 1)
            chunk(CHUNKS - 1, (CHUNKS - 1) % 2, CHUNKS - 2, None)
            for n in range(LN_OPS):
                norm_op(CHUNKS - 1, n)

        @block.tensor
        def _(pe):
            def transpose_rows(c, step):
                pe.wait_ge(gathered[step], 16 * GATHERS * (c + 1))
                if not isinstance(c, int) or c * GROUPS + step >= 1:
                    pe.wait_ge(stack_ok, group_no(c, step) - 1)
                for bt in range(BT):
                    last = nc.tensor.transpose(cols_ps[:, bt * 128:(bt + 1) * 128], x_rows[:, step, bt, :], ident[:, :])
                last.then_inc(cols_tp, 1)

            def transpose_halves(c, step):
                pe.wait_ge(x_dup, group_no(c, step))
                pe.wait_ge(cols_ok, group_no(c, step))
                for r in range(SLOTS):
                    for bt in range(BT):
                        rows = x_halves[:, step % 2, bt * SLOTS + r].rearrange("p a h e -> p (a h e)")
                        last = nc.tensor.transpose(stack_ps[:, r, bt * 128:(bt + 1) * 128], rows, ident[:, :])
                last.then_inc(stack_tp, 1)

            def products(c, b, w_ready):
                kind, q, k, step = BATCHES[b]
                if w_ready:
                    pe.wait_ge(w_lo, w_ready)
                if b == first_batch(step):
                    pe.wait_ge(stack_ok, group_no(c, step))
                if not isinstance(c, int) or c * NB + b >= 2:
                    pe.wait_ge(u_ok, batch_no(c, b) - 2)
                w = W_START[b]
                if kind == "full":
                    for r in range(SLOTS):
                        last = nc.tensor.matmul(t_ps[:, b % 2, r], w_stack[:, w + r * TILE:w + (r + 1) * TILE],
                                                x_stack[:, step % 2, r], start=True, stop=True)
                else:
                    for g, group_step in enumerate((step, step - 1)):
                        own = x_stack[:, group_step % 2]
                        nc.tensor.matmul(t_ps[:, b % 2, 2 * g], w_stack[:, w:w + TILE], own[:, 0],
                                         start=True, stop=True)
                        for slot in (1, 2, 3):
                            at = w + TILE + DIAG_WINDOW[slot] * EMB
                            last = nc.tensor.matmul(t_ps[:, b % 2, 2 * g + 1], w_stack[:, at:at + TILE],
                                                    own[:, DIAG_SOURCE[slot]], start=slot == 1, stop=slot == 3)
                        w += TILE + DIAG_B
                last.then_inc(t_ok, 1)

            def sums(c, b):
                pe.wait_ge(u_ok, batch_no(c, b))
                if b == 0 and (not isinstance(c, int) or c > 0):
                    pe.wait_ge(h_out, SLOTS * c)
                for r in range(SLOTS):
                    last = nc.tensor.matmul(h_ps[32 * r:32 * r + DENSE, 0:CB], dw[:, b * SLOTS + r, :],
                                            u[:, b % U_RING, r], start=b == 0, stop=b == NB - 1)
                last.then_inc(summed, 1)

            def mlp_step(c, n):
                if n >= 2:
                    pe.wait_ge(mlp_act, (MLP_STEPS - 1) * c + n - 1)
                if n == 0:
                    pe.wait_ge(h_out, SLOTS * (c + 1))
                    for bt in range(BT):
                        dst = mlp_ps[:, bt * DENSE:(bt + 1) * DENSE]
                        nc.tensor.matmul(dst, h_sums[:, bt * 128:(bt + 1) * 128], gsum[:, :], start=True, stop=False)
                        last = nc.tensor.matmul(dst, ones[:, :], db_row[:, :], start=False, stop=True)
                elif n == 1:
                    pe.wait_ge(ln_op, (c + 1) * LN_OPS)
                    pe.wait_ge(dense_in, 16 * (c + 1))
                    for bt in range(BT):
                        last = nc.tensor.transpose(mlp_ps[0:2 * DENSE, bt * 128:(bt + 1) * 128],
                                                   z_rows[:, bt, :], ident[:, :])
                elif n < 2 + M1:
                    m = n - 2
                    last = nc.tensor.matmul(mlp_ps, w1_sb[:, m * 128:(m + 1) * 128], z_cols[:, :],
                                            start=True, stop=True)
                elif n < 2 + M1 + M2:
                    m = n - 2 - M1
                    for k in range(M1):
                        last = nc.tensor.matmul(mlp_ps, w2_sb[:, k, m * 128:(m + 1) * 128], hid1[:, k, :],
                                                start=k == 0, stop=k == M1 - 1)
                else:
                    for k in range(M2):
                        last = nc.tensor.matmul(mlp_ps[0:1, :], w3_sb[:, k:k + 1], hid2[:, k, :],
                                                start=k == 0, stop=k == M2 - 1)
                last.then_inc(mlp_mm, 1)

            def chunk(c, before, after):
                for b in range(NB):
                    products(c, b, -(-W_START[b + 1] // STAGE) if before is None else 0)
                    if b >= 2:
                        sums(c, b - 2)
                    elif before is not None:
                        sums(before, NB - 2 + b)
                    if before is not None and b in MLP_AT:
                        mlp_step(before, MLP_AT[b])
                    for step in PREP_AT.get(b, []):
                        if step < GROUPS:
                            transpose_rows(c, step)
                        elif after is not None:
                            transpose_rows(after, step - GROUPS)
                    for step in TP_AT.get(b, []):
                        if step < GROUPS:
                            transpose_halves(c, step)
                        elif after is not None:
                            transpose_halves(after, step - GROUPS)

            pe.wait_ge(ident_in, 16)
            for step in range(2):
                transpose_rows(0, step)
                transpose_halves(0, step)
            pe.wait_ge(dw_in, 16 * SLOTS)
            chunk(0, None, 1)
            pe.wait_ge(mlp_in, 16 * 9)
            pe.wait_ge(memset_ok, 2)
            with pe.Fori(1, CHUNKS - 1) as c:
                chunk(c, c - 1, c + 1)
            chunk(CHUNKS - 1, CHUNKS - 2, None)
            for b in (NB - 2, NB - 1):
                sums(CHUNKS - 1, b)
            for n in range(MLP_STEPS):
                mlp_step(CHUNKS - 1, n)


def pair_layout():
    out = []
    for b, (kind, q, k, _) in enumerate(BATCHES):
        w = W_START[b]
        if kind == "full":
            for r in range(SLOTS):
                for s in range(SLOTS):
                    out.append((w + r * TILE + s * EMB, b * SLOTS + r, s, SLOTS * q + r, SLOTS * k + s))
        else:
            for g in range(2):
                base = SLOTS * (q + g)
                for s in (1, 2, 3):
                    out.append((w + s * EMB, b * SLOTS + 2 * g, s, base, base + s))
                for s in (1, 2, 3):
                    at = w + TILE + (DIAG_WINDOW[s] + s) * EMB
                    out.append((at, b * SLOTS + 2 * g + 1, s, base + DIAG_SOURCE[s], base + s))
                w += TILE + DIAG_B
    return out


def kernel(**inputs):
    import numpy as np
    import concourse.bacc as bacc
    from concourse.bass_utils import run_bass_kernel_spmd

    arr = {k: np.asarray(v) for k, v in inputs.items()}
    order = position_order()
    w_in, dense_in = arr["L0_rec_W"], arr["L0_rec_dense_w"]
    w_pairs = np.zeros((EMB, W_COLS), np.float32)
    dense_w = np.zeros((SLOTS, NB * SLOTS, DENSE), np.float32)
    for col, tile, slot, i, j in pair_layout():
        fi, fj = order[i], order[j]
        lo, hi = min(fi, fj), max(fi, fj)
        pair = lo * (FIELDS - 1) - lo * (lo - 1) // 2 + hi - lo - 1
        w_pairs[:, col:col + EMB] = w_in[pair] if fi < fj else w_in[pair].T
        dense_w[slot, tile] = dense_in[pair]
    fields = [order[SLOTS * (GROUPS - 1 - s) + r] for s in range(GROUPS) for r in range(SLOTS)]
    ids = arr["ids"][:, fields].reshape(CHUNKS, BT, 128, FIELDS).transpose(0, 2, 3, 1)
    ids = np.ascontiguousarray(ids.reshape(CHUNKS, 128, FIELDS * BT))
    data = {
        "ids": ids,
        "dense_ctx": arr["dense_ctx"].reshape(CHUNKS, CB, DENSE),
        **{f"tbl_{f}": arr[f"tbl_{f}"] for f in range(FIELDS)},
        "w_pairs": w_pairs,
        "dense_w": dense_w,
        "dense_b": arr["L0_rec_dense_b"].reshape(1, DENSE),
        "gamma": arr["L0_rec_gamma"].reshape(1, DENSE),
        "beta": arr["L0_rec_beta"].reshape(1, DENSE),
        "eye": np.eye(128, dtype=np.float32),
        "group_sum": np.tile(np.eye(32, DENSE, dtype=np.float32), (SLOTS, 1)),
        "w1": arr["W_top1"],
        "b1": np.ascontiguousarray(arr["b_top1"].reshape(M1, 128).T),
        "w2": arr["W_top2"],
        "b2": np.ascontiguousarray(arr["b_top2"].reshape(M2, 128).T),
        "w3": np.ascontiguousarray(arr["W_top3"].reshape(M2, 128).T),
    }
    nc = bacc.Bacc("TRN2", target_bir_lowering=False, num_devices=1)
    arrays, aps = {}, {}
    for name, a in data.items():
        arrays[f"in_{name}"] = np.ascontiguousarray(a)
        aps[name] = nc.dram_tensor(f"in_{name}", a.shape, mybir.dt.from_np(a.dtype), kind="ExternalInput").ap()
    out = nc.dram_tensor("out", (CHUNKS, CB), F32, kind="ExternalOutput").ap()
    tower(nc, aps["ids"], aps["dense_ctx"], [aps[f"tbl_{f}"] for f in range(FIELDS)], aps["w_pairs"],
          aps["dense_w"], aps["dense_b"], aps["gamma"], aps["beta"], aps["eye"], aps["group_sum"],
          aps["w1"], aps["b1"], aps["w2"], aps["b2"], aps["w3"], out)
    r = run_bass_kernel_spmd(nc, [arrays], core_ids=[0])
    return r.results[0]["out"].reshape(BATCH, 1)
```

```python
import concourse.bass as bass
import concourse.mybir as mybir
from concourse.alu_op_type import AluOpType as ALU
from contextlib import ExitStack

F32 = mybir.dt.float32
F32R = mybir.dt.float32r
I32 = mybir.dt.int32
BF16 = mybir.dt.bfloat16
FP16 = mybir.dt.float16
ACT = mybir.ActivationFunctionType
AX = mybir.AxisListType

FIELDS, EMB, DENSE, BATCH = 40, 32, 16, 2048
LN_EPS = 1e-3
SLOTS = 4
GROUPS = FIELDS // SLOTS
CB = 256
BT = CB // 128
CHUNKS = BATCH // CB
GATHERS = SLOTS * BT
HID1, HID2 = 512, 256
M1, M2 = HID1 // 128, HID2 // 128
TILE = SLOTS * EMB
DIAG_B = 9 * EMB
PICK_STEPS = 1
PICKS = PICK_STEPS * SLOTS
PICK_ROWS = 1000
PICK_P = 125
PICK_V = PICK_ROWS // PICK_P
PARTS = 3
TILES = BATCH // 128
LEAD = (0, 1, 2, 3, 3, 3, 2, 1, 1, 0)
MAX_LEAD = max(LEAD)
WSTAGE = 850
STAGE = 4 * WSTAGE


def position_order():
    return list(range(FIELDS))


def batches_of_chunk():
    out = []
    for step in range(GROUPS):
        q = GROUPS - 1 - step
        if step % 2:
            out.append(("diag", q, q, step))
        partners = [n for n in range(step) if step - n > LEAD[step]] \
            + [n for n in range(step + 1, GROUPS) if n - step <= LEAD[n]]
        out += [("full", q, GROUPS - 1 - other, step) for other in partners]
    return out


BATCHES = batches_of_chunk()
NB = len(BATCHES)
W_WIDTH = {"full": SLOTS * TILE, "diag": 2 * (TILE + DIAG_B)}
W_START = [sum(W_WIDTH[b[0]] for b in BATCHES[:n]) for n in range(NB + 1)]
W_COLS = W_START[-1]
PIECES = W_COLS // STAGE
assert PIECES * STAGE == W_COLS and NB == 50
DIAG_WINDOW = {1: 0, 2: 2, 3: 5}
DIAG_SOURCE = {1: 3, 2: 1, 3: 2}


def first_batch(step):
    return min([n for n, b in enumerate(BATCHES) if b[3] == step], default=None)


def last_batch(step):
    if step % 2 == 0:
        return first_batch(step + 1)
    return max(n for n, b in enumerate(BATCHES) if b[3] == step)


T_RING = 3
U_RING = 4


def slots_of_chunk(ring, swapped):
    turn, out = list(range(ring)), []
    for b in range(NB):
        out.append(turn.pop(1 if b in swapped else 0))
        turn.append(out[-1])
    assert turn == list(range(ring))
    return out


T_SLOT = slots_of_chunk(T_RING, (14, 30))
U_SLOT = slots_of_chunk(U_RING, (8, 19, 33, 44))


def slot_age(b, slots):
    return min(age for age in range(1, NB) if slots[(b - age) % NB] == slots[b])


PREP = {1: (None, None, None, None, 0, 1), 2: (None, None, 1, None, 4, 5), 3: (2, 2, 5, None, 7, 8),
        4: (6, 6, 9, 2, 10, 11), 5: (9, 9, 12, 6, 13, 14), 6: (12, 12, 15, 12, 16, 18),
        7: (17, 17, 20, 19, 21, 23), 8: (25, 25, 28, 26, 29, 31), 9: (33, 33, 36, 34, 37, 38),
        10: (35, 35, 39, 35, 41, 43), 11: (40, 40, 44, 40, None, None),
        12: (45, 45, None, 45, None, None), 13: (None, None, None, 48, None, None)}
HI, LO, AGAIN, COLS, STACK0, STACK1 = range(6)
MLP_KINDS = [("rows", 0)] + [("turn", 0)] + [("layer1", m) for m in range(0, M1, 2)] \
    + [("layer2", m) for m in range(2 * M2)] + [("layer3", 0)]
MLP_STEPS = len(MLP_KINDS)
MLP_NEEDS = {"turn": 0, "layer1": 1, "layer2": 1 + M1 // 2, "layer3": MLP_STEPS - 2}
MLP_AT = dict(zip((3, 20, 22, 24, 27, 30, 32, 36, 46), range(MLP_STEPS)))
HSUM_AT = 3
LN_OPS = 10
ROOT_OP = 5
LN_AT = {5 + n + (2 if n > ROOT_OP else 0): n for n in range(LN_OPS)}
ROOT_AT = 5 + ROOT_OP + 1
INDEX_SPLIT = (PICK_STEPS + GROUPS) // 2
PIECE_AT = {0: 0, 1: 1, 2: 2, 3: 3}
FIRST_PIECES = len(PIECE_AT) + 1
DW_EARLY = NB * SLOTS - BATCH // DENSE
DW_LATE_AT = DW_EARLY // SLOTS
assert len(MLP_AT) == MLP_STEPS and max(LN_AT) < 20 and BATCH % DENSE == 0


def groups_for_batches():
    out, latest = {}, -1
    for b, (kind, q, k, _) in enumerate(BATCHES):
        need = GROUPS - 1 - min(q if kind == "diag" else k, k)
        if need > latest:
            out[b] = latest = need
    return out


COLS_FOR = groups_for_batches()


def steps_at(b, what):
    return [step for step, at in sorted(PREP.items()) if at[what] == b]


def side_uses(with_mlp, with_next):
    out = []
    for b in range(NB):
        if with_mlp and b in MLP_AT:
            out.append(("mlp", MLP_AT[b]))
        out += [("stack", step, half) for half in (0, 1) for step in steps_at(b, STACK0 + half)
                if step < GROUPS or with_next]
        out += [("cols", step) for step in steps_at(b, COLS) if step < GROUPS or with_next]
    return out


def pick_field(t):
    return position_order()[SLOTS * (GROUPS - 1 - t // SLOTS) + t % SLOTS]


def pieces_before(b):
    return min(PIECES, -(-W_START[b + 1] // STAGE) + 2)


def tower(nc, ids, pick_ids, iota, scratch, dense_ctx, tables, w_pairs, dense_w, dense_b, gamma, beta, eye, group_sum,
          w1, b1, w2, b2, w3, out):
    order = position_order()
    ctx = ExitStack()
    with ctx:
        def sb(name, shape, dt=F32):
            return ctx.enter_context(nc.sbuf_tensor(name, shape, dt))

        def sem(name):
            return ctx.enter_context(nc.semaphore(name))

        w_stack = sb("w_stack", [128, W_COLS], F32R)
        w_raw = sb("w_raw", [128, 2, WSTAGE])
        w_high = sb("w_high", [128, 2, WSTAGE], F32R)
        dw = sb("dw", [128, NB * SLOTS, DENSE])
        index = sb("index", [128, (GROUPS - PICK_STEPS) * GATHERS], I32)
        x_rows = sb("x_rows", [128, GROUPS, BT, TILE])
        x_halves = sb("x_halves", [128, 2, BT * SLOTS, 2, 2, EMB], F32R)
        x_stack = sb("x_stack", [128, 2, SLOTS, CB], F32R)
        x_cols = sb("x_cols", [128, 2 * GROUPS, CB])
        u = sb("u", [128, U_RING, SLOTS, CB])
        ident = sb("ident", [128, 128])
        ident_r = sb("ident_r", [128, 128], F32R)
        gsum = sb("gsum", [128, DENSE])
        ones = sb("ones", [1, 128])
        db_row = sb("db_row", [1, DENSE])
        gamma_b = sb("gamma_b", [128, DENSE])
        beta_b = sb("beta_b", [128, DENSE])
        w1_sb = sb("w1_sb", [2 * DENSE, HID1])
        w2_sb = sb("w2_sb", [128, M1, HID2])
        w3_sb = sb("w3_sb", [128, M2])
        b1_sb = sb("b1_sb", [128, M1])
        b2_sb = sb("b2_sb", [128, M2])
        h_sums = sb("h_sums", [128, CB])
        h_rows = sb("h_rows", [128, BT, DENSE])
        ln_sum = sb("ln_sum", [128, BT])
        ln_mean = sb("ln_mean", [128, BT])
        ln_cent = sb("ln_cent", [128, BT, DENSE])
        ln_sq = sb("ln_sq", [128, BT, DENSE])
        ln_var = sb("ln_var", [128, BT])
        ln_ve = sb("ln_ve", [128, BT])
        ln_root = sb("ln_root", [128, BT])
        ln_rstd = sb("ln_rstd", [128, BT])
        ln_z = sb("ln_z", [128, BT, DENSE])
        ln_g = sb("ln_g", [128, BT, DENSE])
        z_rows = sb("z_rows", [128, BT, 2 * DENSE])
        z_cols = sb("z_cols", [2 * DENSE, CB])
        hid = w_raw[:, :, :].rearrange("p a n -> p (a n)")
        hid1 = hid[:, 0:M1 * CB].rearrange("p (m n) -> p m n", m=M1)
        hid2 = hid[:, M1 * CB:(M1 + M2) * CB].rearrange("p (m n) -> p m n", m=M2)
        y_row = sb("y_row", [1, CB])

        iota_sb = sb("iota_sb", [128, PICK_V])
        pool_cols = x_cols[0:PICK_P, :, :].rearrange("p a n -> p (a n)")
        n_parts = PICKS * PICK_V * PARTS * EMB
        parts = pool_cols[:, 0:n_parts // 2].bitcast(BF16).rearrange("p (t v s e) -> p t v s e", t=PICKS, v=PICK_V, s=PARTS)
        pick_table = pool_cols[:, n_parts // 2:n_parts // 2 + PICKS * PICK_V * EMB].rearrange(
            "p (t v e) -> p t v e", t=PICKS, v=PICK_V)
        own_cols = x_cols[:, GROUPS:2 * GROUPS, :].rearrange("p a n -> p (a n)")
        picked = own_cols[:, 0:TILES * TILE].rearrange("p (t r e) -> p t r e", t=TILES, r=SLOTS)
        part_rest = own_cols[0:PICK_P, TILES * TILE:GROUPS * CB].rearrange("p (i v e) -> p i v e", i=2, v=PICK_V)
        assert n_parts // 2 + PICKS * PICK_V * EMB <= GROUPS * CB
        one_hot = [u[0:PICK_P, i, :, :].rearrange("p a n -> p (a n)").bitcast(BF16) for i in range(U_RING)]
        dw_flat = dw[:, :, :].rearrange("p t d -> p (t d)")
        dw_flat = dw_flat[:, DW_EARLY * DENSE:]
        pick_ids_sb = dw_flat[0:PICKS, 0:BATCH].bitcast(I32)
        wide_ids = [dw_flat[:, i * BATCH // 2:(i + 1) * BATCH // 2].bitcast(FP16) for i in range(2)]
        ids_r = w_stack[0:PICKS, W_COLS - BATCH:W_COLS]
        select_r = w_stack[0:PICKS, W_COLS - BATCH - PICKS * 128:W_COLS - BATCH].rearrange("k (t m) -> k t m", t=PICKS)
        assert BATCH + PICKS * 128 <= STAGE

        t_ps = ctx.enter_context(nc.psum_tensor("t_ps", [128, T_RING, SLOTS, CB], F32))
        side_ps = ctx.enter_context(nc.psum_tensor("side_ps", [128, 512], F32))
        h_ps = ctx.enter_context(nc.psum_tensor("h_ps", [128, 512], F32))
        picks_ps = t_ps[:, 0:2, :, :].rearrange("p a r n -> p (a r n)").rearrange("p (k n) -> p k n", k=4)
        picks_ps = picks_ps[:, :, 0:4 * PARTS * EMB].rearrange("p k (t s e) -> p k t s e", t=4, s=PARTS)
        wide_ps = t_ps[:, 2, :, :].rearrange("p r n -> p (r n)")


        def last_ps(n):
            flat = t_ps[:, :, :, :].rearrange("p a r n -> p (a r n)")
            at = n % (2 * T_RING) * 512
            return flat[:, at:at + 512]

        index_hi, index_lo = sem("index_hi"), sem("index_lo")
        gathered = [sem(f"gathered{s}") for s in range(GROUPS)]
        staged = [sem(f"staged{i}") for i in range(2)]
        w_in = [sem(f"w_in{i}") for i in range(2)]
        dw_in, dw_late_in, ident_in, mlp_in = sem("dw_in"), sem("dw_late_in"), sem("ident_in"), sem("mlp_in")
        gather_turn = sem("gather_turn")
        pick_ids_in, tables_in, iota_in = sem("pick_ids_in"), sem("tables_in"), sem("iota_in")
        ids_ok, wide_mm, wide_ok = sem("ids_ok"), sem("wide_mm"), sem("wide_ok")
        part_h, part_hr, part_m, part_l = sem("part_h"), sem("part_hr"), sem("part_m"), sem("part_l")
        hot, hot_used, pick_high, pick_add, pick_sum = sem("hot"), sem("hot_used"), sem("pick_high"), sem("pick_add"), sem("pick_sum")
        stored = sem("stored")
        dense_in, y_out = sem("dense_in"), sem("y_out")
        w_hi, w_lo = sem("w_hi"), sem("w_lo")
        x_hi, x_lo, x_dup = sem("x_hi"), sem("x_lo"), sem("x_dup")
        cols_tp, stack_tp = sem("cols_tp"), sem("stack_tp")
        cols_ok, stack_ok = sem("cols_ok"), sem("stack_ok")
        t_ok, u_ok, summed = sem("t_ok"), sem("u_ok"), sem("summed")
        h_out = sem("h_out")
        memset_ok = sem("memset_ok")
        mlp_mm, mlp_act, ln_op, root = sem("mlp_mm"), sem("mlp_act"), sem("ln_op"), sem("root")

        block = ctx.enter_context(nc.Block())

        small = [(gsum[:, :], group_sum), (db_row[:, :], dense_b), (gamma_b[:, :], gamma.to_broadcast([128, DENSE])),
                 (beta_b[:, :], beta.to_broadcast([128, DENSE])), (w1_sb[:, :], w1),
                 (w2_sb[:, :, :], w2.rearrange("(k p) n -> p k n", p=128)),
                 (w3_sb[:, :], w3), (b1_sb[:, :], b1), (b2_sb[:, :], b2)]

        def batch_no(c, b):
            return c * NB + b + 1

        def group_no(c, step):
            return c * GROUPS + step + 1

        def stack_no(c, step, half):
            return 2 * (c * GROUPS + step) + half + 1

        def mlp_no(c, n):
            return c * MLP_STEPS + n + 1

        def first(c):
            return isinstance(c, int) and c == 0

        def rows_of(c, step):
            if first(c) and step < PICK_STEPS:
                return picked[:, 0:BT, :, :].rearrange("p b s e -> p b (s e)")
            return x_rows[:, step % GROUPS, :, :]

        def rows_in(c, step):
            return 16 * c if step < PICK_STEPS else 16 * (c + 1) * GATHERS

        @block.gpsimd
        def _(pool):
            def gather(c, step):
                if step == PICK_STEPS:
                    pool.wait_ge(index_hi, 16 * (c + 1))
                if step == INDEX_SPLIT:
                    pool.wait_ge(index_lo, 16 * (c + 1))
                if not isinstance(c, int):
                    pool.wait_ge(stack_tp, stack_no(c - 1, step, 1))
                    pool.sem_inc(gather_turn, 1)
                for r in range(SLOTS):
                    table = tables[order[SLOTS * (GROUPS - 1 - step) + r]]
                    for bt in range(BT):
                        n = (step - PICK_STEPS) * GATHERS + r * BT + bt
                        pool.indirect_dma_start(
                            x_rows[:, step, bt, r * EMB:(r + 1) * EMB], None, table,
                            bass.IndirectOffsetOnAxis(ap=index[:, n:n + 1], axis=0),
                        ).then_inc(gathered[step], 16)

            for step in range(PICK_STEPS, GROUPS):
                gather(0, step)
            with pool.Fori(1, CHUNKS) as c:
                for step in range(PICK_STEPS, GROUPS):
                    gather(c, step)

        @block.sync
        def _(sp):
            half = (INDEX_SPLIT - PICK_STEPS) * GATHERS

            def load_indices(c, lo):
                if not isinstance(c, int) or c > 0:
                    for step in range(INDEX_SPLIT, GROUPS) if lo else range(PICK_STEPS, INDEX_SPLIT):
                        sp.wait_ge(gathered[step], rows_in(c - 1, step))
                src = ids[bass.ds(c, 1)].rearrange("a p n -> p (a n)")
                part = slice(half, None) if lo else slice(0, half)
                sp.dma_start(index[:, part], src[:, part]).then_inc(index_lo if lo else index_hi, 16)

            def load_piece(n):
                if n >= 2:
                    sp.wait_ge(w_in[n % 2], 256 * (n // 2))
                sp.dma_start(w_raw[:, n % 2, :], w_pairs[n]).then_inc(staged[n % 2], 16)

            def copy_piece(n):
                sp.wait_ge(w_lo, n + 1)
                if n == PIECES - 1:
                    sp.wait_ge(wide_ok, 4 * PICKS)
                for quarter in range(4):
                    if quarter == 2 and 1 <= n < PIECES - 1:
                        load_piece(n + 1)
                    at = n * STAGE + quarter * WSTAGE
                    for part in range(4):
                        half_of = w_high[:, n % 2, :] if part < 2 else w_raw[:, n % 2, :]
                        sp.dma_start(w_stack[part * EMB:(part + 1) * EMB, at:at + WSTAGE].bitcast(F32),
                                     half_of[quarter * EMB:(quarter + 1) * EMB, :].bitcast(F32)).then_inc(w_in[n % 2], 16)

            def load_picked(c):
                sp.wait_ge(stack_tp, stack_no(c - 1, 0, 1))
                sp.dma_start(x_rows[:, 0, :, :].rearrange("p b n -> p (b n)"),
                             scratch[bass.ds(c, 1)].rearrange("a p n -> p (a n)")).then_inc(gathered[0], 16)

            def load_dense_w(tiles, done):
                for s in range(SLOTS):
                    sp.dma_start(dw[s * EMB:(s + 1) * EMB, tiles, :],
                                 dense_w[s:s + 1, tiles].to_broadcast([EMB, tiles.stop - tiles.start, DENSE]))\
                      .then_inc(done, 16)

            load_indices(0, 0)
            sp.dma_start(pick_ids_sb, pick_ids).then_inc(pick_ids_in, 16)
            sp.dma_start(ident[:, :], eye).then_inc(ident_in, 16)
            for t in range(PICKS):
                sp.dma_start(pick_table[:, t], tables[pick_field(t)].rearrange("(p v) e -> p v e", v=PICK_V))\
                  .then_inc(tables_in, 16)
                if t == 0:
                    sp.dma_start(iota_sb[:, :], iota).then_inc(iota_in, 16)
            load_indices(0, 1)
            load_piece(0)
            load_piece(1)
            load_dense_w(slice(0, DW_EARLY), dw_in)
            for n in range(FIRST_PIECES - 1):
                copy_piece(n)
                if n == 2:
                    load_indices(1, 0)
            sp.wait_ge(pick_sum, 2 * PICKS)
            sp.dma_start(scratch.rearrange("c p n -> p c n"),
                         picked.rearrange("p (c b) r e -> p c (b r e)", b=BT)).then_inc(stored, 16)
            copy_piece(FIRST_PIECES - 1)
            sp.wait_ge(hot, PICK_V * PICKS)
            load_dense_w(slice(DW_EARLY, NB * SLOTS), dw_late_in)
            sp.wait_ge(stored, 16)
            load_picked(1)
            load_indices(1, 1)
            for n in range(FIRST_PIECES, PIECES):
                copy_piece(n)
            for dst, src in small:
                sp.dma_start(dst, src).then_inc(mlp_in, 16)
            with sp.Fori(2, CHUNKS) as c:
                load_indices(c, 0)
                load_indices(c, 1)
                load_picked(c)

        @block.scalar
        def _(act):
            def split_piece(n):
                act.wait_ge(staged[n % 2], 16 * (n // 2 + 1))
                nc.scalar.activation(w_high[:, n % 2, :], w_raw[:, n % 2, :], ACT.Copy).then_inc(w_hi, 1)

            def widen_ids(t):
                if t >= 2:
                    act.wait_ge(hot, PICK_V * (t - 1))
                for k in range(4):
                    act.wait_ge(wide_mm, 4 * t + k + 1)
                    nc.scalar.activation(wide_ids[t % 2][:, k * 512:(k + 1) * 512],
                                         wide_ps[:, (k % 2) * 512:(k % 2 + 1) * 512], ACT.Copy).then_inc(wide_ok, 1)

            def split_table(t):
                act.wait_ge(tables_in, 16 * PICKS)
                nc.scalar.activation(parts[:, t, :, 0, :], pick_table[:, t], ACT.Copy).then_inc(part_h, 1)
                act.wait_ge(part_hr, t + 1)
                nc.scalar.activation(parts[:, t, :, 1, :], part_rest[:, t % 2], ACT.Copy).then_inc(part_m, 1)

            def high_picked(t):
                act.wait_ge(hot_used, PICK_V * (t + 1))
                own = picked[:, :, t, :].rearrange("p (k t) e -> p k t e", k=4)
                for i in range(2):
                    ks = slice(2 * i, 2 * i + 2)
                    nc.scalar.activation(own[:, ks], picks_ps[:, ks, :, 0, :], ACT.Copy).then_inc(pick_high, 1)

            def high_half(c, step):
                own = x_halves[:, step % 2]
                rows = rows_of(c, step).rearrange("p b (s e) -> p (b s) e", e=EMB)
                if first(c) and step == 0:
                    act.wait_ge(pick_sum, 2 * PICKS)
                else:
                    act.wait_ge(gathered[step % GROUPS], rows_in(c + step // GROUPS, step % GROUPS))
                if not first(c) or step >= 2:
                    act.wait_ge(stack_tp, stack_no(c, step - 2, 1))
                nc.scalar.activation(own[:, :, :, 0, :],
                                     rows.unsqueeze(2).to_broadcast([128, BT * SLOTS, 2, EMB]),
                                     ACT.Copy).then_inc(x_hi, 1)

            def low_again(c, step):
                own = x_halves[:, step % 2]
                act.wait_ge(x_lo, group_no(c, step))
                nc.scalar.activation(own[:, :, 1, 1, :], own[:, :, 0, 1, :],
                                     ACT.Copy).then_inc(x_dup, 1)

            def cols_out(c, step, parity):
                block_no = (parity if step < GROUPS else 1 - parity) * GROUPS + GROUPS - 1 - step % GROUPS
                act.wait_ge(cols_tp, group_no(c, step))
                nc.scalar.activation(x_cols[:, bass.ds(block_no, 1), :].rearrange("p a n -> p (a n)"),
                                     side_ps[:, 0:CB], ACT.Copy).then_inc(cols_ok, 1)

            def stack_out(c, step, half):
                act.wait_ge(stack_tp, stack_no(c, step, half))
                if half == 0 and (not first(c) or step >= 2):
                    act.wait_ge(t_ok, batch_no(c, last_batch(step - 2) if step >= 2
                                               else last_batch(step - 2 + GROUPS) - NB))
                nc.scalar.activation(x_stack[:, step % 2, 2 * half:2 * half + 2, :],
                                     side_ps[:, :].rearrange("p (r n) -> p r n", r=2), ACT.Copy).then_inc(stack_ok, 1)

            def sums_out(c):
                act.wait_ge(summed, batch_no(c, NB - 1))
                nc.scalar.activation(h_sums[:, :], h_ps[:, 0:CB], ACT.Copy).then_inc(h_out, 1)

            def load_dense(c):
                act.dma_start(z_rows[:, :, DENSE:2 * DENSE],
                              dense_ctx[bass.ds(c, 1)].rearrange("a (b p) n -> p (a b) n", p=128))\
                   .then_inc(dense_in, 16)

            def norm_root(c):
                act.wait_ge(ln_op, c * LN_OPS + ROOT_OP + 1)
                nc.scalar.activation(ln_root[:, :], ln_ve[:, :], ACT.Sqrt).then_inc(root, 1)

            def mlp_step(c, n, ps):
                kind, m = MLP_KINDS[n]
                act.wait_ge(mlp_mm, mlp_no(c, n))
                if kind == "rows":
                    op = nc.scalar.activation(h_rows[:, :, :], ps[:, 0:BT * DENSE]
                                              .rearrange("p (b d) -> p b d", d=DENSE), ACT.Copy)
                elif kind == "turn":
                    op = nc.scalar.activation(z_cols[:, :], ps[0:2 * DENSE, 0:CB], ACT.Copy)
                elif kind == "layer1":
                    for i in range(2):
                        op = nc.scalar.activation(hid1[:, m + i, :], ps[:, i * CB:(i + 1) * CB], ACT.Relu,
                                                  bias=b1_sb[:, m + i:m + i + 1])
                elif kind == "layer2":
                    at = m % 2 * 128
                    op = nc.scalar.activation(hid2[:, m // 2, at:at + 128], ps[:, 0:128], ACT.Relu,
                                              bias=b2_sb[:, m // 2:m // 2 + 1])
                else:
                    op = nc.scalar.activation(y_row[:, :], ps[0:1, 0:CB], ACT.Copy)
                op.then_inc(mlp_act, 1)
                if kind == "layer3":
                    act.wait_ge(mlp_act, mlp_no(c, n))
                    act.dma_start(out[bass.ds(c, 1), :], y_row[:, :]).then_inc(y_out, 16)

            def chunk(c, parity, before, after):
                pieces = FIRST_PIECES
                for b in range(NB):
                    if before is None:
                        while pieces < pieces_before(b):
                            split_piece(pieces)
                            pieces += 1
                    elif b == HSUM_AT:
                        sums_out(before)
                        load_dense(before)
                    if before is not None and b == ROOT_AT:
                        norm_root(before)
                    if before is not None and b in MLP_AT:
                        mlp_step(before, MLP_AT[b], side_ps)
                    for half in (0, 1):
                        for step in steps_at(b, STACK0 + half):
                            if step < GROUPS or after is not None:
                                stack_out(c, step, half)
                    for step in steps_at(b, HI):
                        if step < GROUPS or after is not None:
                            high_half(c, step)
                    for step in steps_at(b, COLS):
                        if step < GROUPS or after is not None:
                            cols_out(c, step, parity)
                    for step in steps_at(b, AGAIN):
                        if step < GROUPS or after is not None:
                            low_again(c, step)
                if before is not None:
                    act.wait_ge(y_out, 16 * (before + 1))

            act.wait_ge(pick_ids_in, 16)
            nc.scalar.activation(ids_r, pick_ids_sb, ACT.Copy).then_inc(ids_ok, 1)
            act.wait_ge(ident_in, 16)
            nc.scalar.activation(select_r, ident[0:PICKS, 0:PICKS].unsqueeze(2).to_broadcast([PICKS, PICKS, 128]),
                                 ACT.Copy).then_inc(ids_ok, 1)
            nc.scalar.activation(ident_r[:, :], ident[:, :], ACT.Copy).then_inc(ids_ok, 1)
            act.wait_ge(ids_ok, 3)
            split_table(0)
            widen_ids(0)
            for t in range(PICKS):
                if t >= 1:
                    high_picked(t - 1)
                if t + 1 < PICKS:
                    split_table(t + 1)
                    widen_ids(t + 1)
                if t in PIECE_AT:
                    split_piece(PIECE_AT[t])
            high_picked(PICKS - 1)
            high_half(0, 0)
            cols_out(0, 0, 0)
            low_again(0, 0)
            high_half(0, 1)
            for half in (0, 1):
                stack_out(0, 0, half)
            low_again(0, 1)
            high_half(0, 2)
            for step in range(1, MAX_LEAD + 1):
                cols_out(0, step, 0)
            split_piece(FIRST_PIECES - 1)
            chunk(0, 0, None, 1)
            act.wait_ge(mlp_in, 16 * len(small))
            act.wait_ge(memset_ok, 3)
            nc.scalar.activation(ln_root[:, :], ln_ve[:, :], ACT.Sqrt)
            with act.Fori(1, CHUNKS - 1) as c:
                chunk(c, c % 2, c - 1, c + 1)
            chunk(CHUNKS - 1, (CHUNKS - 1) % 2, CHUNKS - 2, None)
            sums_out(CHUNKS - 1)
            load_dense(CHUNKS - 1)
            for n in range(MLP_STEPS):
                mlp_step(CHUNKS - 1, n, last_ps(n))
                if n == 0:
                    norm_root(CHUNKS - 1)
            act.wait_ge(y_out, 16 * CHUNKS)

        @block.vector
        def _(dve):
            def split_piece(n):
                dve.wait_ge(w_hi, n + 1)
                nc.vector.tensor_tensor(w_raw[:, n % 2, :].bitcast(F32R), w_raw[:, n % 2, :], w_high[:, n % 2, :],
                                        ALU.subtract).then_inc(w_lo, 1)

            def split_table(t):
                dve.wait_ge(part_h, t + 1)
                nc.vector.tensor_tensor(part_rest[:, t % 2], pick_table[:, t], parts[:, t, :, 0, :],
                                        ALU.subtract).then_inc(part_hr, 1)

            def low_part(t):
                dve.wait_ge(part_m, t + 1)
                nc.vector.tensor_tensor(parts[:, t, :, 2, :], part_rest[:, t % 2], parts[:, t, :, 1, :],
                                        ALU.subtract).then_inc(part_l, 1)

            def one_hots(t, v):
                n = t * PICK_V + v
                if n >= U_RING:
                    dve.wait_ge(hot_used, n - U_RING + 1)
                nc.vector.tensor_scalar(one_hot[n % U_RING], wide_ids[t % 2][0:PICK_P, :],
                                        iota_sb[0:PICK_P, v:v + 1], None, ALU.is_equal).then_inc(hot, 1)

            def sum_parts(t):
                own = picked[:, :, t, :].rearrange("p (k t) e -> p k t e", k=4)
                for i in range(2):
                    ks = slice(2 * i, 2 * i + 2)
                    dve.wait_ge(pick_high, 2 * t + i + 1)
                    nc.vector.tensor_tensor(own[:, ks], own[:, ks], picks_ps[:, ks, :, 1, :],
                                            ALU.add).then_inc(pick_add, 1)
                for i in range(2):
                    ks = slice(2 * i, 2 * i + 2)
                    dve.wait_ge(pick_add, 2 * t + i + 1)
                    nc.vector.tensor_tensor(own[:, ks], own[:, ks], picks_ps[:, ks, :, 2, :],
                                            ALU.add).then_inc(pick_sum, 1)

            def lo_half(c, step):
                own = x_halves[:, step % 2]
                rows = rows_of(c, step).rearrange("p b (s e) -> p (b s) e", e=EMB)
                dve.wait_ge(x_hi, group_no(c, step))
                nc.vector.tensor_tensor(own[:, :, 0, 1, :], rows,
                                        own[:, :, 0, 0, :], ALU.subtract).then_inc(x_lo, 1)

            def multiply(c, b, parity):
                kind, q, k, step = BATCHES[b]
                dve.wait_ge(t_ok, batch_no(c, b))
                if b in COLS_FOR:
                    dve.wait_ge(cols_ok, group_no(c, COLS_FOR[b]))
                if not first(c) or b >= slot_age(b, U_SLOT):
                    dve.wait_ge(summed, batch_no(c, b) - slot_age(b, U_SLOT))
                if kind == "full":
                    x = x_cols[:, bass.ds(parity * GROUPS + k, 1), :].to_broadcast([128, SLOTS, CB])
                    nc.vector.tensor_tensor(u[:, U_SLOT[b]], t_ps[:, T_SLOT[b]], x, ALU.mult).then_inc(u_ok, 1)
                else:
                    x = x_cols[:, bass.ds(parity * GROUPS + q, 2), :].unsqueeze(2).to_broadcast([128, 2, 2, CB])
                    nc.vector.tensor_tensor(u[:, U_SLOT[b]].rearrange("p (g a) n -> p g a n", a=2),
                                            t_ps[:, T_SLOT[b]].rearrange("p (g a) n -> p g a n", a=2),
                                            x, ALU.mult).then_inc(u_ok, 1)

            def over_rows(ap):
                return ap.unsqueeze(1).to_broadcast([128, BT, DENSE])

            def over_dense(ap):
                return ap.unsqueeze(2).to_broadcast([128, BT, DENSE])

            def norm_op(c, n):
                if n == 0:
                    dve.wait_ge(mlp_act, mlp_no(c, 0))
                else:
                    dve.wait_ge(ln_op, c * LN_OPS + n)
                if n == 0:
                    op = nc.vector.tensor_reduce(ln_sum[:, :], h_rows[:, :, :], AX.X, ALU.add)
                elif n == 1:
                    op = nc.vector.tensor_scalar(ln_mean[:, :], ln_sum[:, :], 1.0 / DENSE, None, ALU.mult)
                elif n == 2:
                    op = nc.vector.tensor_tensor(ln_cent[:, :, :], h_rows[:, :, :], over_dense(ln_mean[:, :]), ALU.subtract)
                elif n == 3:
                    op = nc.vector.tensor_tensor(ln_sq[:, :, :], ln_cent[:, :, :], ln_cent[:, :, :], ALU.mult)
                elif n == 4:
                    op = nc.vector.tensor_reduce(ln_var[:, :], ln_sq[:, :, :], AX.X, ALU.add)
                elif n == 5:
                    op = nc.vector.tensor_scalar(ln_ve[:, :], ln_var[:, :], 1.0 / DENSE, LN_EPS, ALU.mult, ALU.add)
                elif n == 6:
                    dve.wait_ge(root, c + 1)
                    op = nc.vector.reciprocal(ln_rstd[:, :], ln_root[:, :])
                elif n == 7:
                    op = nc.vector.tensor_tensor(ln_z[:, :, :], ln_cent[:, :, :], over_dense(ln_rstd[:, :]), ALU.mult)
                elif n == 8:
                    op = nc.vector.tensor_tensor(ln_g[:, :, :], ln_z[:, :, :], over_rows(gamma_b[:, :]), ALU.mult)
                else:
                    op = nc.vector.tensor_tensor(z_rows[:, :, 0:DENSE], ln_g[:, :, :], over_rows(beta_b[:, :]), ALU.add)
                op.then_inc(ln_op, 1)

            def chunk(c, parity, before, after):
                pieces = FIRST_PIECES
                for b in range(NB):
                    if before is None:
                        while pieces < pieces_before(b):
                            split_piece(pieces)
                            pieces += 1
                    multiply(c, b, parity)
                    if before is not None and b in LN_AT:
                        norm_op(before, LN_AT[b])
                    for step in steps_at(b, LO):
                        if step < GROUPS or after is not None:
                            lo_half(c, step)

            nc.vector.memset(h_ps[:, 0:CB], 0.0).then_inc(memset_ok, 1)
            nc.vector.memset(ones[:, :], 1.0).then_inc(memset_ok, 1)
            nc.vector.memset(ln_ve[:, :], 1.0).then_inc(memset_ok, 1)
            dve.wait_ge(iota_in, 16)
            split_table(0)
            low_part(0)
            for t in range(PICKS):
                dve.wait_ge(wide_ok, 4 * (t + 1))
                for v in range(PICK_V):
                    one_hots(t, v)
                    if v == 1 and t >= 1:
                        sum_parts(t - 1)
                    if v == 0 and t + 1 < PICKS:
                        split_table(t + 1)
                    if v == 4 and t + 1 < PICKS:
                        low_part(t + 1)
                    if v == 5 and t in PIECE_AT:
                        split_piece(PIECE_AT[t])
            sum_parts(PICKS - 1)
            for step in range(3):
                lo_half(0, step)
            split_piece(FIRST_PIECES - 1)
            chunk(0, 0, None, 1)
            dve.wait_ge(mlp_in, 16 * len(small))
            with dve.Fori(1, CHUNKS - 1) as c:
                chunk(c, c % 2, c - 1, c + 1)
            chunk(CHUNKS - 1, (CHUNKS - 1) % 2, CHUNKS - 2, None)
            for n in range(LN_OPS):
                norm_op(CHUNKS - 1, n)

        @block.tensor
        def _(pe):
            def side_free(c, uses, n):
                if n > 0:
                    use = uses[n - 1]
                    if use[0] == "cols":
                        pe.wait_ge(cols_ok, group_no(c, use[1]))
                    elif use[0] == "stack":
                        pe.wait_ge(stack_ok, stack_no(c, use[1], use[2]))
                    else:
                        pe.wait_ge(mlp_act, mlp_no(c - 1, use[1]))

            def transpose_rows(c, step):
                if first(c) and step == 0:
                    pe.wait_ge(pick_sum, 2 * PICKS)
                else:
                    pe.wait_ge(gathered[step % GROUPS], rows_in(c + step // GROUPS, step % GROUPS))
                for bt in range(BT):
                    last = nc.tensor.transpose(side_ps[:, bt * 128:(bt + 1) * 128], rows_of(c, step)[:, bt, :],
                                               ident[:, :])
                last.then_inc(cols_tp, 1)

            def transpose_halves(c, step, half):
                pe.wait_ge(x_dup, group_no(c, step))
                for r in (0, 1):
                    for bt in range(BT):
                        rows = x_halves[:, step % 2, bt * SLOTS + 2 * half + r].rearrange("p a h e -> p (a h e)")
                        at = r * CB + bt * 128
                        last = nc.tensor.transpose(side_ps[:, at:at + 128].bitcast(F32R), rows,
                                                   ident_r[:, :])
                last.then_inc(stack_tp, 1)

            def products(c, b, w_ready):
                kind, q, k, step = BATCHES[b]
                for n in range(max(w_ready - 2, 0), w_ready):
                    pe.wait_ge(w_in[n % 2], 256 * (n // 2 + 1))
                if b == first_batch(step):
                    pe.wait_ge(stack_ok, stack_no(c, step, 1))
                if not first(c) or b >= slot_age(b, T_SLOT):
                    pe.wait_ge(u_ok, batch_no(c, b) - slot_age(b, T_SLOT))
                w = W_START[b]
                if kind == "full":
                    for r in range(SLOTS):
                        last = nc.tensor.matmul(t_ps[:, T_SLOT[b], r], w_stack[:, w + r * TILE:w + (r + 1) * TILE],
                                                x_stack[:, step % 2, r], start=True, stop=True)
                else:
                    for g, group_step in enumerate((step, step - 1)):
                        own = x_stack[:, group_step % 2]
                        nc.tensor.matmul(t_ps[:, T_SLOT[b], 2 * g], w_stack[:, w:w + TILE], own[:, 0],
                                         start=True, stop=True)
                        for slot in (1, 2, 3):
                            at = w + TILE + DIAG_WINDOW[slot] * EMB
                            last = nc.tensor.matmul(t_ps[:, T_SLOT[b], 2 * g + 1], w_stack[:, at:at + TILE],
                                                    own[:, DIAG_SOURCE[slot]], start=slot == 1, stop=slot == 3)
                        w += TILE + DIAG_B
                last.then_inc(t_ok, 1)

            def sums(c, b):
                pe.wait_ge(u_ok, batch_no(c, b))
                if first(c) and b == DW_LATE_AT:
                    pe.wait_ge(dw_late_in, 16 * SLOTS)
                if b == 0 and (not isinstance(c, int) or c > 0):
                    pe.wait_ge(h_out, c)
                for r in range(SLOTS):
                    last = nc.tensor.matmul(h_ps[32 * r:32 * r + DENSE, 0:CB], dw[:, b * SLOTS + r, :],
                                            u[:, U_SLOT[b], r], start=b == 0, stop=b == NB - 1)
                last.then_inc(summed, 1)

            def mlp_step(c, n, ps):
                kind, m = MLP_KINDS[n]
                if n >= 1:
                    pe.wait_ge(mlp_act, mlp_no(c, MLP_NEEDS[kind]))
                if kind == "rows":
                    pe.wait_ge(h_out, c + 1)
                    for bt in range(BT):
                        dst = ps[:, bt * DENSE:(bt + 1) * DENSE]
                        nc.tensor.matmul(dst, h_sums[:, bt * 128:(bt + 1) * 128], gsum[:, :], start=True, stop=False)
                        last = nc.tensor.matmul(dst, ones[:, :], db_row[:, :], start=False, stop=True)
                elif kind == "turn":
                    pe.wait_ge(ln_op, (c + 1) * LN_OPS)
                    pe.wait_ge(dense_in, 16 * (c + 1))
                    for bt in range(BT):
                        last = nc.tensor.transpose(ps[0:2 * DENSE, bt * 128:(bt + 1) * 128],
                                                   z_rows[:, bt, :], ident[:, :])
                elif kind == "layer1":
                    for i in range(2):
                        last = nc.tensor.matmul(ps[:, i * CB:(i + 1) * CB],
                                                w1_sb[:, (m + i) * 128:(m + i + 1) * 128], z_cols[:, :],
                                                start=True, stop=True)
                elif kind == "layer2":
                    at = m % 2 * 128
                    for k in range(M1):
                        last = nc.tensor.matmul(ps[:, 0:128], w2_sb[:, k, m // 2 * 128:(m // 2 + 1) * 128],
                                                hid1[:, k, at:at + 128], start=k == 0, stop=k == M1 - 1)
                else:
                    for k in range(M2):
                        last = nc.tensor.matmul(ps[0:1, 0:CB], w3_sb[:, k:k + 1], hid2[:, k, :],
                                                start=k == 0, stop=k == M2 - 1)
                last.then_inc(mlp_mm, 1)

            def chunk(c, before, after):
                uses = side_uses(before is not None, after is not None)
                n = 0
                if before is None:
                    pe.wait_ge(memset_ok, 3)
                pe.wait_ge(cols_ok, group_no(c, MAX_LEAD))
                for b in range(NB):
                    if b % 2 == 0:
                        for ahead in (b, b + 1):
                            products(c, ahead, -(-W_START[ahead + 1] // STAGE) if before is None else 0)
                    else:
                        for behind in (4, 3):
                            if b >= behind:
                                sums(c, b - behind)
                            elif before is not None:
                                sums(before, NB + b - behind)
                    if before is not None and b in MLP_AT:
                        side_free(c, uses, n)
                        mlp_step(before, MLP_AT[b], side_ps)
                        n += 1
                    for half in (0, 1):
                        for step in steps_at(b, STACK0 + half):
                            if step < GROUPS or after is not None:
                                side_free(c, uses, n)
                                transpose_halves(c, step, half)
                                n += 1
                    for step in steps_at(b, COLS):
                        if step < GROUPS or after is not None:
                            side_free(c, uses, n)
                            transpose_rows(c, step)
                            n += 1
                assert n == len(uses)

            def spread_ids(t, ks):
                for k in ks:
                    if 4 * t + k >= 2:
                        pe.wait_ge(wide_ok, 4 * t + k - 1)
                    nc.tensor.matmul(wide_ps[:, (k % 2) * 512:(k % 2 + 1) * 512], select_r[:, t, :],
                                     ids_r[:, k * 512:(k + 1) * 512], start=True, stop=True).then_inc(wide_mm, 1)

            def pick(t):
                if t + 1 < PICKS:
                    spread_ids(t + 1, (0, 1))
                pe.wait_ge(part_l, t + 1)
                for v in range(PICK_V):
                    n = t * PICK_V + v
                    pe.wait_ge(hot, n + 1)
                    rows = parts[:, t, v].rearrange("p s e -> p (s e)")
                    for i in range(TILES):
                        if v == 0 and t >= 1 and i % (TILES // 2) == 0:
                            pe.wait_ge(pick_sum, 2 * t - 1 + i // (TILES // 2))
                        last = nc.tensor.matmul(picks_ps[:, i // 4, i % 4].rearrange("p s e -> p (s e)"),
                                                one_hot[n % U_RING][:, i * 128:(i + 1) * 128], rows,
                                                start=v == 0 and i % 4 == 0, stop=v == PICK_V - 1 and i % 4 == 3)
                    last.then_inc(hot_used, 1)
                    if v == 0 and t + 1 < PICKS:
                        spread_ids(t + 1, (2, 3))

            pe.wait_ge(ids_ok, 3)
            spread_ids(0, range(4))
            for t in range(PICKS):
                pick(t)
            transpose_rows(0, 0)
            pe.wait_ge(cols_ok, group_no(0, 0))
            transpose_halves(0, 0, 0)
            pe.wait_ge(stack_ok, stack_no(0, 0, 0))
            transpose_halves(0, 0, 1)
            pe.wait_ge(stack_ok, stack_no(0, 0, 1))
            for step in range(1, MAX_LEAD + 1):
                transpose_rows(0, step)
                if step < MAX_LEAD:
                    pe.wait_ge(cols_ok, group_no(0, step))
            pe.wait_ge(dw_in, 16 * SLOTS)
            chunk(0, None, 1)
            pe.wait_ge(mlp_in, 16 * len(small))
            with pe.Fori(1, CHUNKS - 1) as c:
                chunk(c, c - 1, c + 1)
            chunk(CHUNKS - 1, CHUNKS - 2, None)
            for b in range(NB - 3, NB):
                sums(CHUNKS - 1, b)
            for n in range(MLP_STEPS):
                mlp_step(CHUNKS - 1, n, last_ps(n))


def pair_layout():
    out = []
    for b, (kind, q, k, _) in enumerate(BATCHES):
        w = W_START[b]
        if kind == "full":
            for r in range(SLOTS):
                for s in range(SLOTS):
                    out.append((w + r * TILE + s * EMB, b * SLOTS + r, s, SLOTS * q + r, SLOTS * k + s))
        else:
            for g in range(2):
                base = SLOTS * (q + g)
                for s in (1, 2, 3):
                    out.append((w + s * EMB, b * SLOTS + 2 * g, s, base, base + s))
                for s in (1, 2, 3):
                    at = w + TILE + (DIAG_WINDOW[s] + s) * EMB
                    out.append((at, b * SLOTS + 2 * g + 1, s, base + DIAG_SOURCE[s], base + s))
                w += TILE + DIAG_B
    return out


def kernel(**inputs):
    import numpy as np
    import concourse.bacc as bacc
    from concourse.bass_utils import run_bass_kernel_spmd

    arr = {k: np.asarray(v) for k, v in inputs.items()}
    order = position_order()
    w_in, dense_in = arr["L0_rec_W"], arr["L0_rec_dense_w"]
    w_pairs = np.zeros((EMB, W_COLS), np.float32)
    pick_fields = [pick_field(t) for t in range(PICKS)]
    assert all(arr[f"tbl_{f}"].shape == (PICK_ROWS, EMB) for f in pick_fields)
    dense_w = np.zeros((SLOTS, NB * SLOTS, DENSE), np.float32)
    for col, tile, slot, i, j in pair_layout():
        fi, fj = order[i], order[j]
        lo, hi = min(fi, fj), max(fi, fj)
        pair = lo * (FIELDS - 1) - lo * (lo - 1) // 2 + hi - lo - 1
        w_pairs[:, col:col + EMB] = w_in[pair] if fi < fj else w_in[pair].T
        dense_w[slot, tile] = dense_in[pair]
    fields = [order[SLOTS * (GROUPS - 1 - s) + r] for s in range(PICK_STEPS, GROUPS) for r in range(SLOTS)]
    ids = arr["ids"][:, fields].reshape(CHUNKS, BT, 128, len(fields)).transpose(0, 2, 3, 1)
    ids = np.ascontiguousarray(ids.reshape(CHUNKS, 128, len(fields) * BT))
    w_pairs = w_pairs.reshape(EMB, PIECES, 4, WSTAGE).transpose(1, 2, 0, 3).reshape(PIECES, 128, WSTAGE)
    data = {
        "ids": ids,
        "pick_ids": arr["ids"][:, pick_fields].T,
        "iota": np.minimum(np.arange(128)[:, None] * PICK_V + np.arange(PICK_V), PICK_ROWS).astype(np.float32),
        "dense_ctx": arr["dense_ctx"].reshape(CHUNKS, CB, DENSE),
        **{f"tbl_{f}": arr[f"tbl_{f}"] for f in range(FIELDS)},
        "w_pairs": w_pairs,
        "dense_w": dense_w,
        "dense_b": arr["L0_rec_dense_b"].reshape(1, DENSE),
        "gamma": arr["L0_rec_gamma"].reshape(1, DENSE),
        "beta": arr["L0_rec_beta"].reshape(1, DENSE),
        "eye": np.eye(128, dtype=np.float32),
        "group_sum": np.tile(np.eye(32, DENSE, dtype=np.float32), (SLOTS, 1)),
        "w1": arr["W_top1"],
        "b1": np.ascontiguousarray(arr["b_top1"].reshape(M1, 128).T),
        "w2": arr["W_top2"],
        "b2": np.ascontiguousarray(arr["b_top2"].reshape(M2, 128).T),
        "w3": np.ascontiguousarray(arr["W_top3"].reshape(M2, 128).T),
    }
    nc = bacc.Bacc("TRN2", target_bir_lowering=False, num_devices=1)
    arrays, aps = {}, {}
    for name, a in data.items():
        arrays[f"in_{name}"] = np.ascontiguousarray(a)
        aps[name] = nc.dram_tensor(f"in_{name}", a.shape, mybir.dt.from_np(a.dtype), kind="ExternalInput").ap()
    out = nc.dram_tensor("out", (CHUNKS, CB), F32, kind="ExternalOutput").ap()
    scratch = nc.dram_tensor("scratch", (CHUNKS, 128, BT * TILE), F32, kind="Internal").ap()
    tower(nc, aps["ids"], aps["pick_ids"], aps["iota"], scratch, aps["dense_ctx"], [aps[f"tbl_{f}"] for f in range(FIELDS)], aps["w_pairs"],
          aps["dense_w"], aps["dense_b"], aps["gamma"], aps["beta"], aps["eye"], aps["group_sum"],
          aps["w1"], aps["b1"], aps["w2"], aps["b2"], aps["w3"], out)
    r = run_bass_kernel_spmd(nc, [arrays], core_ids=[0])
    return r.results[0]["out"].reshape(BATCH, 1)
```

```python
import concourse.bass as bass
import concourse.mybir as mybir
from concourse.alu_op_type import AluOpType as ALU
from contextlib import ExitStack

F32 = mybir.dt.float32
F32R = mybir.dt.float32r
I32 = mybir.dt.int32
BF16 = mybir.dt.bfloat16
FP16 = mybir.dt.float16
ACT = mybir.ActivationFunctionType
AX = mybir.AxisListType

FIELDS, EMB, DENSE, BATCH = 40, 32, 16, 2048
LN_EPS = 1e-3
SLOTS = 4
GROUPS = FIELDS // SLOTS
CB = 256
BT = CB // 128
CHUNKS = BATCH // CB
HID1, HID2 = 512, 256
M1, M2 = HID1 // 128, HID2 // 128
TILE = SLOTS * EMB
DIAG_B = 9 * EMB
PICKS = 5
PICK_STEPS = PICKS // SLOTS
PICKED_STEPS = -(-PICKS // SLOTS)
PICK_ROWS = 1000
PICK_P = 125
PICK_V = PICK_ROWS // PICK_P
PARTS = 3
TILES = BATCH // 128
LEAD = (0, 1, 2, 3, 3, 3, 2, 1, 1, 0)
MAX_LEAD = max(LEAD)
WSTAGE = 850
STAGE = 4 * WSTAGE


def position_order():
    return list(range(FIELDS))


def batches_of_chunk():
    out = []
    for step in range(GROUPS):
        q = GROUPS - 1 - step
        if step % 2:
            out.append(("diag", q, q, step))
        partners = [n for n in range(step) if step - n > LEAD[step]] \
            + [n for n in range(step + 1, GROUPS) if n - step <= LEAD[n]]
        out += [("full", q, GROUPS - 1 - other, step) for other in partners]
    return out


BATCHES = batches_of_chunk()
NB = len(BATCHES)
W_WIDTH = {"full": SLOTS * TILE, "diag": 2 * (TILE + DIAG_B)}
W_START = [sum(W_WIDTH[b[0]] for b in BATCHES[:n]) for n in range(NB + 1)]
W_COLS = W_START[-1]
PIECES = W_COLS // STAGE
assert PIECES * STAGE == W_COLS and NB == 50
DIAG_WINDOW = {1: 0, 2: 2, 3: 5}
DIAG_SOURCE = {1: 3, 2: 1, 3: 2}


def first_batch(step):
    return min([n for n, b in enumerate(BATCHES) if b[3] == step], default=None)


def last_batch(step):
    if step % 2 == 0:
        return first_batch(step + 1)
    return max(n for n, b in enumerate(BATCHES) if b[3] == step)


T_RING = 3
U_RING = 5
HOT_RING = 4


def slots_of_chunk(ring, swapped):
    turn, out = list(range(ring)), []
    for b in range(NB):
        out.append(turn.pop(1 if b in swapped else 0))
        turn.append(out[-1])
    assert turn == list(range(ring))
    return out


T_SLOT = slots_of_chunk(T_RING, (14, 30))
U_SLOT = slots_of_chunk(U_RING, ())


def slot_age(b, slots):
    return min(age for age in range(1, NB) if slots[(b - age) % NB] == slots[b])


PREP = {1: (None, None, None, None, 0, 1), 2: (None, None, 1, None, 4, 5), 3: (2, 2, 5, None, 7, 8),
        4: (6, 6, 9, 2, 10, 11), 5: (9, 9, 12, 6, 13, 14), 6: (12, 12, 15, 12, 16, 18),
        7: (17, 17, 20, 19, 21, 23), 8: (25, 26, 29, 26, 30, 31), 9: (33, 34, 36, 34, 37, 38),
        10: (35, 35, 39, 39, 41, 42), 11: (40, 40, 43, 40, None, None),
        12: (44, 44, None, 43, None, None), 13: (None, None, None, 48, None, None)}
HI, LO, AGAIN, COLS, STACK0, STACK1 = range(6)
MLP_KINDS = [("rows", 0)] + [("turn", 0)] + [("layer1", m) for m in range(M1)] \
    + [("layer2", m) for m in range(2 * M2)] + [("layer3", 0)]
MLP_STEPS = len(MLP_KINDS)
MLP_PLACES = ((3,), (20,), (22,), (24,), (25,), (27,), (28, 29), (32, 33), (35, 36), (44, 45), (46, 47))
MLP_START = {places[0]: n for n, places in enumerate(MLP_PLACES)}
MLP_END = {places[-1]: n for n, places in enumerate(MLP_PLACES)}
MLP_NEEDS = {"turn": 0, "layer1": 1, "layer2": 1 + M1, "layer3": MLP_STEPS - 2}
HSUM_AT = 2
LN_OPS = 10
ROOT_OP = 5
LN_AT = {5 + n + (2 if n > ROOT_OP else 0): n for n in range(LN_OPS)}
ROOT_AT = 5 + ROOT_OP + 1
INDEX_SPLIT = (PICK_STEPS + GROUPS) // 2
PIECE_AT = {t: t for t in range(PICKS)}
FIRST_PIECES = len(PIECE_AT) + 1
DW_EARLY = NB * SLOTS - BATCH // DENSE
DW_LATE_AT = DW_EARLY // SLOTS
assert len(MLP_PLACES) == MLP_STEPS and max(LN_AT) < 20 and BATCH % DENSE == 0


def groups_for_batches():
    out, latest = {}, -1
    for b, (kind, q, k, _) in enumerate(BATCHES):
        need = GROUPS - 1 - min(q if kind == "diag" else k, k)
        if need > latest:
            out[b] = latest = need
    return out


COLS_FOR = groups_for_batches()


def steps_at(b, what):
    return [step for step, at in sorted(PREP.items()) if at[what] == b]


def side_uses(with_mlp, with_next):
    out = []
    for b in range(NB):
        if with_mlp and b in MLP_START:
            out.append(("mlp", MLP_START[b]))
        out += [("stack", step, half) for half in (0, 1) for step in steps_at(b, STACK0 + half)
                if step < GROUPS or with_next]
        out += [("cols", step) for step in steps_at(b, COLS) if step < GROUPS or with_next]
    return out


def picked_slots(step):
    return min(max(PICKS - SLOTS * step, 0), SLOTS)


GATHERED = [(step, r) for step in range(GROUPS) for r in range(picked_slots(step), SLOTS)]


def pick_field(t):
    return position_order()[SLOTS * (GROUPS - 1 - t // SLOTS) + t % SLOTS]


def pieces_before(b):
    return min(PIECES, -(-W_START[b + 1] // STAGE) + 2)


def tower(nc, ids, pick_ids, iota, scratch, dense_ctx, tables, w_pairs, dense_w, dense_b, gamma, beta, eye, group_sum,
          w1, b1, w2, b2, w3, out):
    order = position_order()
    ctx = ExitStack()
    with ctx:
        def sb(name, shape, dt=F32):
            return ctx.enter_context(nc.sbuf_tensor(name, shape, dt))

        def sem(name):
            return ctx.enter_context(nc.semaphore(name))

        w_stack = sb("w_stack", [128, W_COLS], F32R)
        w_raw = sb("w_raw", [128, 2, WSTAGE])
        w_high = sb("w_high", [128, 2, WSTAGE])
        dw = sb("dw", [128, NB * SLOTS, DENSE])
        index = sb("index", [128, len(GATHERED) * BT], I32)
        x_rows = sb("x_rows", [128, GROUPS, BT, TILE])
        x_halves = sb("x_halves", [128, 2, BT * SLOTS, 2, 2, EMB], F32R)
        x_stack = sb("x_stack", [128, 2, SLOTS, CB], F32R)
        x_cols = sb("x_cols", [128, 2 * GROUPS, CB])
        u = sb("u", [128, U_RING, SLOTS, CB])
        ident = sb("ident", [128, 128])
        ident_r = sb("ident_r", [128, 128], F32R)
        gsum = sb("gsum", [128, DENSE])
        ones = sb("ones", [1, 128])
        db_row = sb("db_row", [1, DENSE])
        gamma_b = sb("gamma_b", [128, DENSE])
        beta_b = sb("beta_b", [128, DENSE])
        w1_sb = sb("w1_sb", [2 * DENSE, HID1])
        w2_sb = sb("w2_sb", [128, M1, HID2])
        w3_sb = sb("w3_sb", [128, M2])
        b1_sb = sb("b1_sb", [128, M1])
        b2_sb = sb("b2_sb", [128, M2])
        h_rows = sb("h_rows", [128, BT, DENSE])
        ln_sum = sb("ln_sum", [128, BT])
        ln_mean = sb("ln_mean", [128, BT])
        ln_cent = sb("ln_cent", [128, BT, DENSE])
        ln_sq = sb("ln_sq", [128, BT, DENSE])
        ln_var = sb("ln_var", [128, BT])
        ln_ve = sb("ln_ve", [128, BT])
        ln_root = sb("ln_root", [128, BT])
        ln_rstd = sb("ln_rstd", [128, BT])
        ln_z = sb("ln_z", [128, BT, DENSE])
        ln_g = sb("ln_g", [128, BT, DENSE])
        z_rows = sb("z_rows", [128, BT, 2 * DENSE])
        hid = w_raw[:, :, :].rearrange("p a n -> p (a n)")
        hid1 = hid[:, 0:M1 * CB].rearrange("p (m n) -> p m n", m=M1)
        hid2 = hid[:, M1 * CB:(M1 + M2) * CB].rearrange("p (m n) -> p m n", m=M2)
        after_w = w_high[:, :, :].rearrange("p a n -> p (a n)")
        h_sums = after_w[:, 0:CB]
        z_cols = after_w[0:2 * DENSE, CB:2 * CB]
        y_row = after_w[0:1, 2 * CB:3 * CB]

        iota_sb = sb("iota_sb", [128, PICK_V])
        cols_flat = x_cols[0:PICK_P, :, :].rearrange("p a n -> p (a n)")
        n_parts = PICKS * PICK_V * PARTS * EMB
        parts = cols_flat[:, 0:n_parts // 2].bitcast(BF16).rearrange(
            "p (t v s e) -> p t v s e", t=PICKS, v=PICK_V, s=PARTS)
        in_u = CB * SLOTS // (PICK_V * EMB)
        u_tables = u[0:PICK_P, U_RING - 1, :, :].rearrange("p a n -> p (a n)").rearrange(
            "p (t v e) -> p t v e", t=in_u, v=PICK_V)
        more_tables = cols_flat[:, n_parts // 2:n_parts // 2 + (PICKS - in_u) * PICK_V * EMB].rearrange(
            "p (t v e) -> p t v e", t=PICKS - in_u, v=PICK_V)
        pick_table = [u_tables[:, t] if t < in_u else more_tables[:, t - in_u] for t in range(PICKS)]
        assert n_parts // 2 + (PICKS - in_u) * PICK_V * EMB <= GROUPS * CB
        part_rest = x_rows[0:PICK_P, 0, :, :].rearrange("p b n -> p (b n)").rearrange("p (v e) -> p v e", v=PICK_V)
        picked = x_cols[:, GROUPS:2 * GROUPS, :].rearrange("p a n -> p (a n)").rearrange(
            "p (t r e) -> p t r e", t=TILES, r=PICKS)
        one_hot = [u[0:PICK_P, i, :, :].rearrange("p a n -> p (a n)").bitcast(BF16) for i in range(HOT_RING)]
        late_dw = dw[:, DW_EARLY:, :].rearrange("p t d -> p (t d)")
        pick_ids_sb = late_dw[0:PICKS, 0:BATCH].bitcast(I32)
        wide_ids = [late_dw[:, i * BATCH // 2:(i + 1) * BATCH // 2].bitcast(FP16) for i in range(2)]
        ids_r = w_stack[0:PICKS, W_COLS - BATCH:W_COLS]
        select_r = w_stack[0:PICKS, W_COLS - BATCH - PICKS * 128:W_COLS - BATCH].rearrange("k (t m) -> k t m", t=PICKS)
        assert BATCH + PICKS * 128 <= STAGE

        t_ps = ctx.enter_context(nc.psum_tensor("t_ps", [128, T_RING, SLOTS, CB], F32))
        side_ps = ctx.enter_context(nc.psum_tensor("side_ps", [128, 512], F32))
        h_ps = ctx.enter_context(nc.psum_tensor("h_ps", [128, 512], F32))
        picks_ps = t_ps[:, 0:2, :, :].rearrange("p a r n -> p (a r n)").rearrange("p (k n) -> p k n", k=4)
        picks_ps = picks_ps[:, :, 0:4 * PARTS * EMB].rearrange("p k (t s e) -> p k t s e", t=4, s=PARTS)
        wide_ps = t_ps[:, 2, :, :].rearrange("p r n -> p (r n)")

        def spare_bank(n):
            flat = t_ps[:, :, :, :].rearrange("p a r n -> p (a r n)")
            at = n % (2 * T_RING) * 512
            return flat[:, at:at + 512]

        index_early, index_late = sem("index_early"), sem("index_late")
        gathered = [sem(f"gathered{s}") for s in range(GROUPS)]
        staged = [sem(f"staged{i}") for i in range(2)]
        w_in = [sem(f"w_in{i}") for i in range(2)]
        dw_in, dw_late_in, ident_in, mlp_in = sem("dw_in"), sem("dw_late_in"), sem("ident_in"), sem("mlp_in")
        gather_turn, index_turn = sem("gather_turn"), sem("index_turn")
        pick_ids_in, tables_in, iota_in = sem("pick_ids_in"), sem("tables_in"), sem("iota_in")
        ids_ok, wide_mm, wide_ok = sem("ids_ok"), sem("wide_mm"), sem("wide_ok")
        part_h, part_hr, part_m, part_l = sem("part_h"), sem("part_hr"), sem("part_m"), sem("part_l")
        hot, hot_used = sem("hot"), sem("hot_used")
        pick_high, pick_add, pick_sum = sem("pick_high"), sem("pick_add"), sem("pick_sum")
        stored = sem("stored")
        picked_in = [sem(f"picked_in{s}") for s in range(PICKED_STEPS)]
        rows_moved = sem("rows_moved")
        dense_in, y_out = sem("dense_in"), sem("y_out")
        w_hi, w_lo = sem("w_hi"), sem("w_lo")
        x_hi, x_lo, x_dup = sem("x_hi"), sem("x_lo"), sem("x_dup")
        cols_tp, stack_tp = sem("cols_tp"), sem("stack_tp")
        cols_ok, stack_ok = sem("cols_ok"), sem("stack_ok")
        t_ok, u_ok, summed = sem("t_ok"), sem("u_ok"), sem("summed")
        h_out = sem("h_out")
        memset_ok = sem("memset_ok")
        mlp_mm, mlp_act, ln_op, root = sem("mlp_mm"), sem("mlp_act"), sem("ln_op"), sem("root")

        block = ctx.enter_context(nc.Block())

        small = [(gsum[:, :], group_sum), (db_row[:, :], dense_b), (gamma_b[:, :], gamma.to_broadcast([128, DENSE])),
                 (beta_b[:, :], beta.to_broadcast([128, DENSE])), (w1_sb[:, :], w1),
                 (w2_sb[:, :, :], w2.rearrange("(k p) n -> p k n", p=128)),
                 (w3_sb[:, :], w3), (b1_sb[:, :], b1), (b2_sb[:, :], b2)]

        def batch_no(c, b):
            return c * NB + b + 1

        def group_no(c, step):
            return c * GROUPS + step + 1

        def stack_no(c, step, half):
            return 2 * (c * GROUPS + step) + half + 1

        def mlp_no(c, n):
            return c * MLP_STEPS + n + 1

        def first(c):
            return isinstance(c, int) and c == 0

        def rows_in(c, step):
            return 16 * BT * (SLOTS - picked_slots(step)) * (c + 1)

        @block.gpsimd
        def _(pool):
            def gather(c, step):
                if step == PICK_STEPS:
                    pool.wait_ge(index_early, 16 * (c + 1))
                if step == INDEX_SPLIT:
                    pool.wait_ge(index_late, 16 * (c + 1))
                if not isinstance(c, int):
                    pool.wait_ge(stack_tp, stack_no(c - 1, step, 1))
                    pool.sem_inc(gather_turn, 1)
                for r in range(picked_slots(step), SLOTS):
                    table = tables[order[SLOTS * (GROUPS - 1 - step) + r]]
                    for bt in range(BT):
                        n = GATHERED.index((step, r)) * BT + bt
                        pool.indirect_dma_start(
                            x_rows[:, step, bt, r * EMB:(r + 1) * EMB], None, table,
                            bass.IndirectOffsetOnAxis(ap=index[:, n:n + 1], axis=0),
                        ).then_inc(gathered[step], 16)

            for step in range(PICK_STEPS, GROUPS):
                gather(0, step)
            with pool.Fori(1, CHUNKS) as c:
                for step in range(PICK_STEPS, GROUPS):
                    gather(c, step)

        @block.sync
        def _(sp):
            half = GATHERED.index((INDEX_SPLIT, 0)) * BT

            def load_indices(c, lo):
                if not isinstance(c, int) or c > 0:
                    for step in range(INDEX_SPLIT, GROUPS) if lo else range(PICK_STEPS, INDEX_SPLIT):
                        sp.wait_ge(gathered[step], rows_in(c - 1, step))
                        if step < PICKED_STEPS:
                            sp.sem_inc(index_turn, 1)
                src = ids[bass.ds(c, 1)].rearrange("a p n -> p (a n)")
                part = slice(half, None) if lo else slice(0, half)
                sp.dma_start(index[:, part], src[:, part]).then_inc(index_late if lo else index_early, 16)

            def load_piece(n):
                if n >= 2:
                    sp.wait_ge(w_in[n % 2], 256 * (n // 2))
                sp.dma_start(w_raw[:, n % 2, :], w_pairs[n]).then_inc(staged[n % 2], 16)

            def copy_piece(n):
                sp.wait_ge(w_lo, n + 1)
                if n == PIECES - 1:
                    sp.wait_ge(wide_ok, 4 * PICKS)
                for quarter in range(4):
                    if quarter == 2 and 1 <= n < PIECES - 1:
                        load_piece(n + 1)
                    at = n * STAGE + quarter * WSTAGE
                    for part in range(4):
                        half_of = w_high[:, n % 2, :] if part < 2 else w_raw[:, n % 2, :]
                        sp.dma_start(w_stack[part * EMB:(part + 1) * EMB, at:at + WSTAGE].bitcast(F32),
                                     half_of[quarter * EMB:(quarter + 1) * EMB, :]).then_inc(w_in[n % 2], 16)

            def load_picked(c):
                sp.wait_ge(stack_tp, stack_no(c - 1, PICKED_STEPS - 1, 1))
                for step in range(PICKED_STEPS):
                    src = scratch[step][:, bass.ds(c, 1)].rearrange("p a b n -> p (a b) n")
                    sp.dma_start(x_rows[:, step, :, 0:picked_slots(step) * EMB], src).then_inc(picked_in[step], 16)

            def load_dense_w(tiles, done):
                for s in range(SLOTS):
                    sp.dma_start(dw[s * EMB:(s + 1) * EMB, tiles, :],
                                 dense_w[s:s + 1, tiles].to_broadcast([EMB, tiles.stop - tiles.start, DENSE]))\
                      .then_inc(done, 16)

            load_indices(0, 0)
            sp.dma_start(pick_ids_sb, pick_ids).then_inc(pick_ids_in, 16)
            sp.dma_start(ident[:, :], eye).then_inc(ident_in, 16)
            for t in range(PICKS):
                sp.dma_start(pick_table[t], tables[pick_field(t)].rearrange("(p v) e -> p v e", v=PICK_V))\
                  .then_inc(tables_in, 16)
                if t == 0:
                    sp.dma_start(iota_sb[:, :], iota).then_inc(iota_in, 16)
            load_indices(0, 1)
            load_piece(0)
            load_piece(1)
            load_dense_w(slice(0, DW_EARLY), dw_in)
            for n in range(FIRST_PIECES - 1):
                copy_piece(n)
                if n == 2:
                    load_indices(1, 0)
            sp.wait_ge(pick_sum, 2 * PICKS)
            for step in range(PICKED_STEPS):
                fields = slice(step * SLOTS, step * SLOTS + picked_slots(step))
                sp.dma_start(scratch[step].rearrange("p c b n -> p (c b) n"),
                             picked[:, :, fields, :].rearrange("p t r e -> p t (r e)")).then_inc(stored, 16)
            copy_piece(FIRST_PIECES - 1)
            sp.wait_ge(hot, PICK_V * PICKS)
            load_dense_w(slice(DW_EARLY, NB * SLOTS), dw_late_in)
            sp.wait_ge(stored, 16 * PICKED_STEPS)
            load_picked(1)
            load_indices(1, 1)
            for n in range(FIRST_PIECES, PIECES):
                copy_piece(n)
            for dst, src in small:
                sp.dma_start(dst, src).then_inc(mlp_in, 16)
            with sp.Fori(2, CHUNKS) as c:
                load_indices(c, 0)
                load_indices(c, 1)
                load_picked(c)

        @block.scalar
        def _(act):
            def split_piece(n):
                act.wait_ge(staged[n % 2], 16 * (n // 2 + 1))
                nc.scalar.activation(w_high[:, n % 2, :].bitcast(F32R), w_raw[:, n % 2, :], ACT.Copy).then_inc(w_hi, 1)

            def widen_ids(t):
                if t >= 2:
                    act.wait_ge(hot, PICK_V * (t - 1))
                for k in range(4):
                    act.wait_ge(wide_mm, 4 * t + k + 1)
                    nc.scalar.activation(wide_ids[t % 2][:, k * 512:(k + 1) * 512],
                                         wide_ps[:, (k % 2) * 512:(k % 2 + 1) * 512], ACT.Copy).then_inc(wide_ok, 1)

            def high_part(t):
                act.wait_ge(tables_in, 16 * PICKS)
                nc.scalar.activation(parts[:, t, :, 0, :], pick_table[t], ACT.Copy).then_inc(part_h, 1)

            def middle_part(t):
                act.wait_ge(part_hr, t + 1)
                nc.scalar.activation(parts[:, t, :, 1, :], part_rest, ACT.Copy).then_inc(part_m, 1)

            def high_picked(t):
                act.wait_ge(hot_used, PICK_V * (t + 1))
                own = picked[:, :, t, :].rearrange("p (k t) e -> p k t e", k=4)
                for i in range(2):
                    ks = slice(2 * i, 2 * i + 2)
                    nc.scalar.activation(own[:, ks], picks_ps[:, ks, :, 0, :], ACT.Copy).then_inc(pick_high, 1)

            def high_half(c, step):
                own = x_halves[:, step % 2]
                rows = x_rows[:, step % GROUPS, :, :].rearrange("p b (s e) -> p (b s) e", e=EMB)
                if first(c) and step < PICKED_STEPS:
                    act.wait_ge(rows_moved, step + 1)
                if step % GROUPS < PICKED_STEPS and not (first(c) and step < GROUPS):
                    act.wait_ge(picked_in[step % GROUPS], 16 * (c + step // GROUPS))
                if step % GROUPS >= PICK_STEPS:
                    act.wait_ge(gathered[step % GROUPS], rows_in(c + step // GROUPS, step % GROUPS))
                if not first(c) or step >= 2:
                    act.wait_ge(stack_tp, stack_no(c, step - 2, 1))
                nc.scalar.activation(own[:, :, :, 0, :],
                                     rows.unsqueeze(2).to_broadcast([128, BT * SLOTS, 2, EMB]),
                                     ACT.Copy).then_inc(x_hi, 1)

            def low_again(c, step):
                own = x_halves[:, step % 2]
                act.wait_ge(x_lo, group_no(c, step))
                nc.scalar.activation(own[:, :, 1, 1, :], own[:, :, 0, 1, :],
                                     ACT.Copy).then_inc(x_dup, 1)

            def cols_out(c, step, parity, ps):
                block_no = (parity if step < GROUPS else 1 - parity) * GROUPS + GROUPS - 1 - step % GROUPS
                act.wait_ge(cols_tp, group_no(c, step))
                nc.scalar.activation(x_cols[:, bass.ds(block_no, 1), :].rearrange("p a n -> p (a n)"),
                                     ps[:, 0:CB], ACT.Copy).then_inc(cols_ok, 1)

            def stack_out(c, step, half, ps):
                act.wait_ge(stack_tp, stack_no(c, step, half))
                if half == 0 and (not first(c) or step >= 2):
                    act.wait_ge(t_ok, batch_no(c, last_batch(step - 2) if step >= 2
                                               else last_batch(step - 2 + GROUPS) - NB))
                nc.scalar.activation(x_stack[:, step % 2, 2 * half:2 * half + 2, :],
                                     ps[:, :].rearrange("p (r n) -> p r n", r=2), ACT.Copy).then_inc(stack_ok, 1)

            def sums_out(c):
                act.wait_ge(summed, batch_no(c, NB - 1))
                nc.scalar.activation(h_sums[:, :], h_ps[:, 0:CB], ACT.Copy).then_inc(h_out, 1)

            def load_dense(c):
                act.dma_start(z_rows[:, :, DENSE:2 * DENSE],
                              dense_ctx[bass.ds(c, 1)].rearrange("a (b p) n -> p (a b) n", p=128))\
                   .then_inc(dense_in, 16)

            def norm_root(c):
                act.wait_ge(ln_op, c * LN_OPS + ROOT_OP + 1)
                nc.scalar.activation(ln_root[:, :], ln_ve[:, :], ACT.Sqrt).then_inc(root, 1)

            def mlp_step(c, n, ps):
                kind, m = MLP_KINDS[n]
                act.wait_ge(mlp_mm, mlp_no(c, n))
                if kind == "rows":
                    op = nc.scalar.activation(h_rows[:, :, :], ps[:, 0:BT * DENSE]
                                              .rearrange("p (b d) -> p b d", d=DENSE), ACT.Copy)
                elif kind == "turn":
                    op = nc.scalar.activation(z_cols[:, :], ps[0:2 * DENSE, 0:CB], ACT.Copy)
                elif kind == "layer1":
                    op = nc.scalar.activation(hid1[:, m, :], ps[:, 0:CB], ACT.Relu, bias=b1_sb[:, m:m + 1])
                elif kind == "layer2":
                    at = m % 2 * 128
                    op = nc.scalar.activation(hid2[:, m // 2, at:at + 128], ps[:, 0:128], ACT.Relu,
                                              bias=b2_sb[:, m // 2:m // 2 + 1])
                else:
                    op = nc.scalar.activation(y_row[:, :], ps[0:1, 0:CB], ACT.Copy)
                op.then_inc(mlp_act, 1)
                if kind == "layer3":
                    act.wait_ge(mlp_act, mlp_no(c, n))
                    act.dma_start(out[bass.ds(c, 1), :], y_row[:, :]).then_inc(y_out, 16)

            def chunk(c, parity, before, after):
                pieces = FIRST_PIECES
                for b in range(NB):
                    if before is None:
                        while pieces < pieces_before(b):
                            split_piece(pieces)
                            pieces += 1
                    elif b == HSUM_AT:
                        sums_out(before)
                        load_dense(before)
                    if before is not None and b == ROOT_AT:
                        norm_root(before)
                    if before is not None and b in MLP_END:
                        mlp_step(before, MLP_END[b], side_ps)
                    for half in (0, 1):
                        for step in steps_at(b, STACK0 + half):
                            if step < GROUPS or after is not None:
                                stack_out(c, step, half, side_ps)
                    for step in steps_at(b, HI):
                        if step < GROUPS or after is not None:
                            high_half(c, step)
                    for step in steps_at(b, COLS):
                        if step < GROUPS or after is not None:
                            cols_out(c, step, parity, side_ps)
                    for step in steps_at(b, AGAIN):
                        if step < GROUPS or after is not None:
                            low_again(c, step)
                if before is not None:
                    act.wait_ge(y_out, 16 * (before + 1))

            act.wait_ge(pick_ids_in, 16)
            nc.scalar.activation(ids_r, pick_ids_sb, ACT.Copy).then_inc(ids_ok, 1)
            act.wait_ge(ident_in, 16)
            nc.scalar.activation(select_r, ident[0:PICKS, 0:PICKS].unsqueeze(2).to_broadcast([PICKS, PICKS, 128]),
                                 ACT.Copy).then_inc(ids_ok, 1)
            nc.scalar.activation(ident_r[:, :], ident[:, :], ACT.Copy).then_inc(ids_ok, 1)
            act.wait_ge(ids_ok, 3)
            high_part(0)
            middle_part(0)
            widen_ids(0)
            for t in range(PICKS):
                if t + 1 < PICKS:
                    high_part(t + 1)
                if t >= 1:
                    high_picked(t - 1)
                if t + 1 < PICKS:
                    middle_part(t + 1)
                    widen_ids(t + 1)
                if t in PIECE_AT:
                    split_piece(PIECE_AT[t])
            high_picked(PICKS - 1)
            act.wait_ge(pick_sum, 2 * PICKS)
            for step in range(PICKED_STEPS):
                n = picked_slots(step)
                rows = picked[:, 0:BT, step * SLOTS:step * SLOTS + n, :]
                nc.scalar.activation(x_rows[:, step, :, 0:n * EMB], rows.rearrange("p b r e -> p b (r e)"),
                                     ACT.Copy).then_inc(rows_moved, 1)
            high_half(0, 0)
            high_half(0, 1)
            cols_out(0, 0, 0, spare_bank(0))
            low_again(0, 0)
            cols_out(0, 1, 0, spare_bank(1))
            for half in (0, 1):
                stack_out(0, 0, half, spare_bank(MAX_LEAD + 1 + half))
            for step in range(2, MAX_LEAD + 1):
                cols_out(0, step, 0, spare_bank(step))
            low_again(0, 1)
            high_half(0, 2)
            split_piece(FIRST_PIECES - 1)
            chunk(0, 0, None, 1)
            act.wait_ge(mlp_in, 16 * len(small))
            act.wait_ge(memset_ok, 3)
            nc.scalar.activation(ln_root[:, :], ln_ve[:, :], ACT.Sqrt)
            with act.Fori(1, CHUNKS - 1) as c:
                chunk(c, c % 2, c - 1, c + 1)
            chunk(CHUNKS - 1, (CHUNKS - 1) % 2, CHUNKS - 2, None)
            sums_out(CHUNKS - 1)
            load_dense(CHUNKS - 1)
            for n in range(MLP_STEPS):
                mlp_step(CHUNKS - 1, n, spare_bank(n))
                if n == 0:
                    norm_root(CHUNKS - 1)
            act.wait_ge(y_out, 16 * CHUNKS)

        @block.vector
        def _(dve):
            def split_piece(n):
                dve.wait_ge(w_hi, n + 1)
                nc.vector.tensor_tensor(w_raw[:, n % 2, :].bitcast(F32R), w_raw[:, n % 2, :],
                                        w_high[:, n % 2, :].bitcast(F32R),
                                        ALU.subtract).then_inc(w_lo, 1)

            def split_table(t):
                dve.wait_ge(part_h, t + 1)
                if t >= 1:
                    dve.wait_ge(part_l, t)
                nc.vector.tensor_tensor(part_rest, pick_table[t], parts[:, t, :, 0, :],
                                        ALU.subtract).then_inc(part_hr, 1)

            def low_part(t):
                dve.wait_ge(part_m, t + 1)
                nc.vector.tensor_tensor(parts[:, t, :, 2, :], part_rest, parts[:, t, :, 1, :],
                                        ALU.subtract).then_inc(part_l, 1)

            def one_hots(t, v):
                n = t * PICK_V + v
                if n >= HOT_RING:
                    dve.wait_ge(hot_used, n - HOT_RING + 1)
                nc.vector.tensor_scalar(one_hot[n % HOT_RING], wide_ids[t % 2][0:PICK_P, :],
                                        iota_sb[0:PICK_P, v:v + 1], None, ALU.is_equal).then_inc(hot, 1)

            def sum_parts(t):
                own = picked[:, :, t, :].rearrange("p (k t) e -> p k t e", k=4)
                for i in range(2):
                    ks = slice(2 * i, 2 * i + 2)
                    dve.wait_ge(pick_high, 2 * t + i + 1)
                    nc.vector.tensor_tensor(own[:, ks], own[:, ks], picks_ps[:, ks, :, 1, :],
                                            ALU.add).then_inc(pick_add, 1)
                    dve.wait_ge(pick_add, 2 * t + i + 1)
                    nc.vector.tensor_tensor(own[:, ks], own[:, ks], picks_ps[:, ks, :, 2, :],
                                            ALU.add).then_inc(pick_sum, 1)

            def lo_half(c, step):
                own = x_halves[:, step % 2]
                rows = x_rows[:, step % GROUPS, :, :].rearrange("p b (s e) -> p (b s) e", e=EMB)
                dve.wait_ge(x_hi, group_no(c, step))
                nc.vector.tensor_tensor(own[:, :, 0, 1, :], rows,
                                        own[:, :, 0, 0, :], ALU.subtract).then_inc(x_lo, 1)

            def multiply(c, b, parity):
                kind, q, k, step = BATCHES[b]
                dve.wait_ge(t_ok, batch_no(c, b))
                if b in COLS_FOR:
                    dve.wait_ge(cols_ok, group_no(c, COLS_FOR[b]))
                if not first(c) or b >= slot_age(b, U_SLOT):
                    dve.wait_ge(summed, batch_no(c, b) - slot_age(b, U_SLOT))
                if kind == "full":
                    x = x_cols[:, bass.ds(parity * GROUPS + k, 1), :].to_broadcast([128, SLOTS, CB])
                    nc.vector.tensor_tensor(u[:, U_SLOT[b]], t_ps[:, T_SLOT[b]], x, ALU.mult).then_inc(u_ok, 1)
                else:
                    x = x_cols[:, bass.ds(parity * GROUPS + q, 2), :].unsqueeze(2).to_broadcast([128, 2, 2, CB])
                    nc.vector.tensor_tensor(u[:, U_SLOT[b]].rearrange("p (g a) n -> p g a n", a=2),
                                            t_ps[:, T_SLOT[b]].rearrange("p (g a) n -> p g a n", a=2),
                                            x, ALU.mult).then_inc(u_ok, 1)

            def over_rows(ap):
                return ap.unsqueeze(1).to_broadcast([128, BT, DENSE])

            def over_dense(ap):
                return ap.unsqueeze(2).to_broadcast([128, BT, DENSE])

            def norm_op(c, n):
                if n == 0:
                    dve.wait_ge(mlp_act, mlp_no(c, 0))
                else:
                    dve.wait_ge(ln_op, c * LN_OPS + n)
                if n == 0:
                    op = nc.vector.tensor_reduce(ln_sum[:, :], h_rows[:, :, :], AX.X, ALU.add)
                elif n == 1:
                    op = nc.vector.tensor_scalar(ln_mean[:, :], ln_sum[:, :], 1.0 / DENSE, None, ALU.mult)
                elif n == 2:
                    op = nc.vector.tensor_tensor(ln_cent[:, :, :], h_rows[:, :, :], over_dense(ln_mean[:, :]),
                                                 ALU.subtract)
                elif n == 3:
                    op = nc.vector.tensor_tensor(ln_sq[:, :, :], ln_cent[:, :, :], ln_cent[:, :, :], ALU.mult)
                elif n == 4:
                    op = nc.vector.tensor_reduce(ln_var[:, :], ln_sq[:, :, :], AX.X, ALU.add)
                elif n == 5:
                    op = nc.vector.tensor_scalar(ln_ve[:, :], ln_var[:, :], 1.0 / DENSE, LN_EPS, ALU.mult, ALU.add)
                elif n == 6:
                    dve.wait_ge(root, c + 1)
                    op = nc.vector.reciprocal(ln_rstd[:, :], ln_root[:, :])
                elif n == 7:
                    op = nc.vector.tensor_tensor(ln_z[:, :, :], ln_cent[:, :, :], over_dense(ln_rstd[:, :]), ALU.mult)
                elif n == 8:
                    op = nc.vector.tensor_tensor(ln_g[:, :, :], ln_z[:, :, :], over_rows(gamma_b[:, :]), ALU.mult)
                else:
                    op = nc.vector.tensor_tensor(z_rows[:, :, 0:DENSE], ln_g[:, :, :], over_rows(beta_b[:, :]), ALU.add)
                op.then_inc(ln_op, 1)

            def chunk(c, parity, before, after):
                pieces = FIRST_PIECES
                for b in range(NB):
                    if before is None:
                        while pieces < pieces_before(b):
                            split_piece(pieces)
                            pieces += 1
                    multiply(c, b, parity)
                    if before is not None and b in LN_AT:
                        norm_op(before, LN_AT[b])
                    for step in steps_at(b, LO):
                        if step < GROUPS or after is not None:
                            lo_half(c, step)

            nc.vector.memset(h_ps[:, 0:CB], 0.0).then_inc(memset_ok, 1)
            nc.vector.memset(ones[:, :], 1.0).then_inc(memset_ok, 1)
            nc.vector.memset(ln_ve[:, :], 1.0).then_inc(memset_ok, 1)
            dve.wait_ge(iota_in, 16)
            split_table(0)
            low_part(0)
            for t in range(PICKS):
                dve.wait_ge(wide_ok, 4 * (t + 1))
                for v in range(PICK_V):
                    one_hots(t, v)
                    if v == 2 and t >= 1:
                        sum_parts(t - 1)
                    if v == 0 and t + 1 < PICKS:
                        split_table(t + 1)
                    if v == 4 and t + 1 < PICKS:
                        low_part(t + 1)
                    if v == 5 and t in PIECE_AT:
                        split_piece(PIECE_AT[t])
            sum_parts(PICKS - 1)
            for step in range(3):
                lo_half(0, step)
            split_piece(FIRST_PIECES - 1)
            chunk(0, 0, None, 1)
            dve.wait_ge(mlp_in, 16 * len(small))
            with dve.Fori(1, CHUNKS - 1) as c:
                chunk(c, c % 2, c - 1, c + 1)
            chunk(CHUNKS - 1, (CHUNKS - 1) % 2, CHUNKS - 2, None)
            for n in range(LN_OPS):
                norm_op(CHUNKS - 1, n)

        @block.tensor
        def _(pe):
            def side_free(c, use):
                if use[0] == "cols":
                    pe.wait_ge(cols_ok, group_no(c, use[1]))
                elif use[0] == "stack":
                    pe.wait_ge(stack_ok, stack_no(c, use[1], use[2]))
                else:
                    pe.wait_ge(mlp_act, mlp_no(c - 1, use[1]))

            def transpose_rows(c, step, ps):
                if first(c) and step < PICKED_STEPS:
                    pe.wait_ge(rows_moved, step + 1)
                if step % GROUPS < PICKED_STEPS and not (first(c) and step < GROUPS):
                    pe.wait_ge(picked_in[step % GROUPS], 16 * (c + step // GROUPS))
                if step % GROUPS >= PICK_STEPS:
                    pe.wait_ge(gathered[step % GROUPS], rows_in(c + step // GROUPS, step % GROUPS))
                for bt in range(BT):
                    last = nc.tensor.transpose(ps[:, bt * 128:(bt + 1) * 128], x_rows[:, step % GROUPS, bt, :],
                                               ident[:, :])
                last.then_inc(cols_tp, 1)

            def transpose_halves(c, step, half, ps):
                pe.wait_ge(x_dup, group_no(c, step))
                for r in (0, 1):
                    for bt in range(BT):
                        rows = x_halves[:, step % 2, bt * SLOTS + 2 * half + r].rearrange("p a h e -> p (a h e)")
                        at = r * CB + bt * 128
                        last = nc.tensor.transpose(ps[:, at:at + 128].bitcast(F32R), rows,
                                                   ident_r[:, :])
                last.then_inc(stack_tp, 1)

            def products(c, b, w_ready):
                kind, q, k, step = BATCHES[b]
                for n in range(max(w_ready - 2, 0), w_ready):
                    pe.wait_ge(w_in[n % 2], 256 * (n // 2 + 1))
                if b == first_batch(step):
                    pe.wait_ge(stack_ok, stack_no(c, step, 1))
                if not first(c) or b >= slot_age(b, T_SLOT):
                    pe.wait_ge(u_ok, batch_no(c, b) - slot_age(b, T_SLOT))
                w = W_START[b]
                if kind == "full":
                    for r in range(SLOTS):
                        last = nc.tensor.matmul(t_ps[:, T_SLOT[b], r], w_stack[:, w + r * TILE:w + (r + 1) * TILE],
                                                x_stack[:, step % 2, r], start=True, stop=True)
                else:
                    for g, group_step in enumerate((step, step - 1)):
                        own = x_stack[:, group_step % 2]
                        nc.tensor.matmul(t_ps[:, T_SLOT[b], 2 * g], w_stack[:, w:w + TILE], own[:, 0],
                                         start=True, stop=True)
                        for slot in (1, 2, 3):
                            at = w + TILE + DIAG_WINDOW[slot] * EMB
                            last = nc.tensor.matmul(t_ps[:, T_SLOT[b], 2 * g + 1], w_stack[:, at:at + TILE],
                                                    own[:, DIAG_SOURCE[slot]], start=slot == 1, stop=slot == 3)
                        w += TILE + DIAG_B
                last.then_inc(t_ok, 1)

            def sums(c, b):
                pe.wait_ge(u_ok, batch_no(c, b))
                if first(c) and b == DW_LATE_AT:
                    pe.wait_ge(dw_late_in, 16 * SLOTS)
                if b == 0 and (not isinstance(c, int) or c > 0):
                    pe.wait_ge(h_out, c)
                for r in range(SLOTS):
                    last = nc.tensor.matmul(h_ps[32 * r:32 * r + DENSE, 0:CB], dw[:, b * SLOTS + r, :],
                                            u[:, U_SLOT[b], r], start=b == 0, stop=b == NB - 1)
                last.then_inc(summed, 1)

            def mlp_step(c, n, ps, share=0, shares=1):
                kind, m = MLP_KINDS[n]
                if n >= 1 and share == 0:
                    pe.wait_ge(mlp_act, mlp_no(c, MLP_NEEDS[kind]))
                if kind == "rows":
                    pe.wait_ge(h_out, c + 1)
                    for bt in range(BT):
                        dst = ps[:, bt * DENSE:(bt + 1) * DENSE]
                        nc.tensor.matmul(dst, h_sums[:, bt * 128:(bt + 1) * 128], gsum[:, :], start=True, stop=False)
                        last = nc.tensor.matmul(dst, ones[:, :], db_row[:, :], start=False, stop=True)
                elif kind == "turn":
                    pe.wait_ge(ln_op, (c + 1) * LN_OPS)
                    pe.wait_ge(dense_in, 16 * (c + 1))
                    for bt in range(BT):
                        last = nc.tensor.transpose(ps[0:2 * DENSE, bt * 128:(bt + 1) * 128],
                                                   z_rows[:, bt, :], ident[:, :])
                elif kind == "layer1":
                    last = nc.tensor.matmul(ps[:, 0:CB], w1_sb[:, m * 128:(m + 1) * 128], z_cols[:, :],
                                            start=True, stop=True)
                elif kind == "layer2":
                    at = m % 2 * 128
                    for k in range(share * M1 // shares, (share + 1) * M1 // shares):
                        last = nc.tensor.matmul(ps[:, 0:128], w2_sb[:, k, m // 2 * 128:(m // 2 + 1) * 128],
                                                hid1[:, k, at:at + 128], start=k == 0, stop=k == M1 - 1)
                else:
                    for k in range(share * M2 // shares, (share + 1) * M2 // shares):
                        last = nc.tensor.matmul(ps[0:1, 0:CB], w3_sb[:, k:k + 1], hid2[:, k, :],
                                                start=k == 0, stop=k == M2 - 1)
                if share == shares - 1:
                    last.then_inc(mlp_mm, 1)

            def chunk(c, before, after):
                uses = side_uses(before is not None, after is not None)

                def take(*use):
                    n = uses.index(use)
                    if n > 0:
                        side_free(c, uses[n - 1])

                def side_work(b):
                    if before is not None:
                        for n, places in enumerate(MLP_PLACES):
                            if b == places[0]:
                                take("mlp", n)
                            if b in places:
                                mlp_step(before, n, side_ps, places.index(b), len(places))
                    for half in (0, 1):
                        for step in steps_at(b, STACK0 + half):
                            if step < GROUPS or after is not None:
                                take("stack", step, half)
                                transpose_halves(c, step, half, side_ps)
                    for step in steps_at(b, COLS):
                        if step < GROUPS or after is not None:
                            take("cols", step)
                            transpose_rows(c, step, side_ps)

                if before is None:
                    pe.wait_ge(memset_ok, 3)
                pe.wait_ge(cols_ok, group_no(c, MAX_LEAD))
                for b in range(0, NB, 2):
                    for ahead in (b, b + 1):
                        products(c, ahead, -(-W_START[ahead + 1] // STAGE) if before is None else 0)
                    if b != HSUM_AT:
                        side_work(b)
                    for n in (b - 3, b - 2):
                        if n >= 0:
                            sums(c, n)
                        elif before is not None:
                            sums(before, NB + n)
                        if b == HSUM_AT and n < 0:
                            side_work(b)
                    side_work(b + 1)

            def spread_ids(t, ks):
                for k in ks:
                    if 4 * t + k >= 2:
                        pe.wait_ge(wide_ok, 4 * t + k - 1)
                    nc.tensor.matmul(wide_ps[:, (k % 2) * 512:(k % 2 + 1) * 512], select_r[:, t, :],
                                     ids_r[:, k * 512:(k + 1) * 512], start=True, stop=True).then_inc(wide_mm, 1)

            def pick(t):
                if t + 1 < PICKS:
                    spread_ids(t + 1, (0, 1))
                pe.wait_ge(part_l, t + 1)
                for v in range(PICK_V):
                    n = t * PICK_V + v
                    pe.wait_ge(hot, n + 1)
                    rows = parts[:, t, v].rearrange("p s e -> p (s e)")
                    for i in range(TILES):
                        if v == 0 and t >= 1 and i % (TILES // 2) == 0:
                            pe.wait_ge(pick_sum, 2 * t - 1 + i // (TILES // 2))
                        last = nc.tensor.matmul(picks_ps[:, i // 4, i % 4].rearrange("p s e -> p (s e)"),
                                                one_hot[n % HOT_RING][:, i * 128:(i + 1) * 128], rows,
                                                start=v == 0 and i % 4 == 0, stop=v == PICK_V - 1 and i % 4 == 3)
                    last.then_inc(hot_used, 1)
                    if v == 0 and t + 1 < PICKS:
                        spread_ids(t + 1, (2, 3))

            pe.wait_ge(ids_ok, 3)
            spread_ids(0, range(4))
            for t in range(PICKS):
                pick(t)
            for step in range(MAX_LEAD + 1):
                transpose_rows(0, step, spare_bank(step))
            for half in (0, 1):
                transpose_halves(0, 0, half, spare_bank(MAX_LEAD + 1 + half))
            pe.wait_ge(dw_in, 16 * SLOTS)
            chunk(0, None, 1)
            pe.wait_ge(mlp_in, 16 * len(small))
            with pe.Fori(1, CHUNKS - 1) as c:
                chunk(c, c - 1, c + 1)
            chunk(CHUNKS - 1, CHUNKS - 2, None)
            for b in range(NB - 3, NB):
                sums(CHUNKS - 1, b)
            for n in range(MLP_STEPS):
                mlp_step(CHUNKS - 1, n, spare_bank(n))


def pair_layout():
    out = []
    for b, (kind, q, k, _) in enumerate(BATCHES):
        w = W_START[b]
        if kind == "full":
            for r in range(SLOTS):
                for s in range(SLOTS):
                    out.append((w + r * TILE + s * EMB, b * SLOTS + r, s, SLOTS * q + r, SLOTS * k + s))
        else:
            for g in range(2):
                base = SLOTS * (q + g)
                for s in (1, 2, 3):
                    out.append((w + s * EMB, b * SLOTS + 2 * g, s, base, base + s))
                for s in (1, 2, 3):
                    at = w + TILE + (DIAG_WINDOW[s] + s) * EMB
                    out.append((at, b * SLOTS + 2 * g + 1, s, base + DIAG_SOURCE[s], base + s))
                w += TILE + DIAG_B
    return out


def kernel(**inputs):
    import numpy as np
    import concourse.bacc as bacc
    from concourse.bass_utils import run_bass_kernel_spmd

    arr = {k: np.asarray(v) for k, v in inputs.items()}
    order = position_order()
    w_in, dense_in = arr["L0_rec_W"], arr["L0_rec_dense_w"]
    w_pairs = np.zeros((EMB, W_COLS), np.float32)
    pick_fields = [pick_field(t) for t in range(PICKS)]
    assert all(arr[f"tbl_{f}"].shape == (PICK_ROWS, EMB) for f in pick_fields)
    dense_w = np.zeros((SLOTS, NB * SLOTS, DENSE), np.float32)
    for col, tile, slot, i, j in pair_layout():
        fi, fj = order[i], order[j]
        lo, hi = min(fi, fj), max(fi, fj)
        pair = lo * (FIELDS - 1) - lo * (lo - 1) // 2 + hi - lo - 1
        w_pairs[:, col:col + EMB] = w_in[pair] if fi < fj else w_in[pair].T
        dense_w[slot, tile] = dense_in[pair]
    fields = [order[SLOTS * (GROUPS - 1 - step) + r] for step, r in GATHERED]
    ids = arr["ids"][:, fields].reshape(CHUNKS, BT, 128, len(fields)).transpose(0, 2, 3, 1)
    ids = np.ascontiguousarray(ids.reshape(CHUNKS, 128, len(fields) * BT))
    w_pairs = w_pairs.reshape(EMB, PIECES, 4, WSTAGE).transpose(1, 2, 0, 3).reshape(PIECES, 128, WSTAGE)
    data = {
        "ids": ids,
        "pick_ids": arr["ids"][:, pick_fields].T,
        "iota": np.minimum(np.arange(128)[:, None] * PICK_V + np.arange(PICK_V), PICK_ROWS).astype(np.float32),
        "dense_ctx": arr["dense_ctx"].reshape(CHUNKS, CB, DENSE),
        **{f"tbl_{f}": arr[f"tbl_{f}"] for f in range(FIELDS)},
        "w_pairs": w_pairs,
        "dense_w": dense_w,
        "dense_b": arr["L0_rec_dense_b"].reshape(1, DENSE),
        "gamma": arr["L0_rec_gamma"].reshape(1, DENSE),
        "beta": arr["L0_rec_beta"].reshape(1, DENSE),
        "eye": np.eye(128, dtype=np.float32),
        "group_sum": np.tile(np.eye(32, DENSE, dtype=np.float32), (SLOTS, 1)),
        "w1": arr["W_top1"],
        "b1": np.ascontiguousarray(arr["b_top1"].reshape(M1, 128).T),
        "w2": arr["W_top2"],
        "b2": np.ascontiguousarray(arr["b_top2"].reshape(M2, 128).T),
        "w3": np.ascontiguousarray(arr["W_top3"].reshape(M2, 128).T),
    }
    nc = bacc.Bacc("TRN2", target_bir_lowering=False, num_devices=1)
    arrays, aps = {}, {}
    for name, a in data.items():
        arrays[f"in_{name}"] = np.ascontiguousarray(a)
        aps[name] = nc.dram_tensor(f"in_{name}", a.shape, mybir.dt.from_np(a.dtype), kind="ExternalInput").ap()
    out = nc.dram_tensor("out", (CHUNKS, CB), F32, kind="ExternalOutput").ap()
    scratch = [nc.dram_tensor(f"scratch{step}", (128, CHUNKS, BT, picked_slots(step) * EMB), F32, kind="Internal").ap()
               for step in range(PICKED_STEPS)]
    tower(nc, aps["ids"], aps["pick_ids"], aps["iota"], scratch, aps["dense_ctx"],
          [aps[f"tbl_{f}"] for f in range(FIELDS)], aps["w_pairs"], aps["dense_w"], aps["dense_b"], aps["gamma"], aps["beta"], aps["eye"], aps["group_sum"],
          aps["w1"], aps["b1"], aps["w2"], aps["b2"], aps["w3"], out)
    r = run_bass_kernel_spmd(nc, [arrays], core_ids=[0])
    return r.results[0]["out"].reshape(BATCH, 1)
```
